# Optimizing a Trainium2 kernel written in Bass

```python
import numpy as np
import jax
import jax.numpy as jnp

def _softmax(x, axis=-1):
    return jax.nn.softmax(x, axis=axis)

def _gelu(x):
    return jax.nn.gelu(x, approximate=True)

def _silu(x):
    return jax.nn.silu(x)

def _sigmoid(x):
    return jax.nn.sigmoid(x)

def _layernorm(x, axis=-1, eps=1e-05):
    m = jnp.mean(x, axis=axis, keepdims=True)
    v = jnp.var(x, axis=axis, keepdims=True)
    return (x - m) / jnp.sqrt(v + eps)

def _scatter_add(tgt, idx, src, axis=0):
    return tgt.at[idx].add(src)

def _segment_sum(src, seg, n):
    return jax.ops.segment_sum(src, seg, n)
kernel_name = 'mk_dlrm_tower_d1_rec_r8_8789d0'

def setup_inputs(seed: int=0):
    np.random.seed(seed)
    _w = jnp.asarray

    def _rec_inputs():
        import jax
        import jax.numpy as jnp
        _tk = jax.random.key(seed)
        dense_ctx = jax.random.normal(jax.random.fold_in(_tk, 190), (1024, 16), jnp.float32)
        ids = jnp.stack([jax.random.randint(jax.random.fold_in(_tk, 200 + f), (1024,), 0, v, jnp.int32) for f, v in enumerate([12500, 125000, 1250, 125000, 1000, 1250, 125000, 1250, 1000, 12500, 125000, 1000, 1000, 125000, 125000, 125000, 1250, 1000, 125000, 125000, 1250, 1250, 1250, 1000, 12500, 1000, 1000, 12500, 1250, 1250, 125000, 12500, 1000, 125000, 125000, 12500, 125000, 12500, 12500])], axis=1)
        tbl_0 = 0.05 * jax.random.normal(jax.random.fold_in(_tk, 500 + 0), (12500, 16), jnp.float32)
        tbl_1 = 0.05 * jax.random.normal(jax.random.fold_in(_tk, 500 + 1), (125000, 16), jnp.float32)
        tbl_2 = 0.05 * jax.random.normal(jax.random.fold_in(_tk, 500 + 2), (1250, 16), jnp.float32)
        tbl_3 = 0.05 * jax.random.normal(jax.random.fold_in(_tk, 500 + 3), (125000, 16), jnp.float32)
        tbl_4 = 0.05 * jax.random.normal(jax.random.fold_in(_tk, 500 + 4), (1000, 16), jnp.float32)
        tbl_5 = 0.05 * jax.random.normal(jax.random.fold_in(_tk, 500 + 5), (1250, 16), jnp.float32)
        tbl_6 = 0.05 * jax.random.normal(jax.random.fold_in(_tk, 500 + 6), (125000, 16), jnp.float32)
        tbl_7 = 0.05 * jax.random.normal(jax.random.fold_in(_tk, 500 + 7), (1250, 16), jnp.float32)
        tbl_8 = 0.05 * jax.random.normal(jax.random.fold_in(_tk, 500 + 8), (1000, 16), jnp.float32)
        tbl_9 = 0.05 * jax.random.normal(jax.random.fold_in(_tk, 500 + 9), (12500, 16), jnp.float32)
        tbl_10 = 0.05 * jax.random.normal(jax.random.fold_in(_tk, 500 + 10), (125000, 16), jnp.float32)
        tbl_11 = 0.05 * jax.random.normal(jax.random.fold_in(_tk, 500 + 11), (1000, 16), jnp.float32)
        tbl_12 = 0.05 * jax.random.normal(jax.random.fold_in(_tk, 500 + 12), (1000, 16), jnp.float32)
        tbl_13 = 0.05 * jax.random.normal(jax.random.fold_in(_tk, 500 + 13), (125000, 16), jnp.float32)
        tbl_14 = 0.05 * jax.random.normal(jax.random.fold_in(_tk, 500 + 14), (125000, 16), jnp.float32)
        tbl_15 = 0.05 * jax.random.normal(jax.random.fold_in(_tk, 500 + 15), (125000, 16), jnp.float32)
        tbl_16 = 0.05 * jax.random.normal(jax.random.fold_in(_tk, 500 + 16), (1250, 16), jnp.float32)
        tbl_17 = 0.05 * jax.random.normal(jax.random.fold_in(_tk, 500 + 17), (1000, 16), jnp.float32)
        tbl_18 = 0.05 * jax.random.normal(jax.random.fold_in(_tk, 500 + 18), (125000, 16), jnp.float32)
        tbl_19 = 0.05 * jax.random.normal(jax.random.fold_in(_tk, 500 + 19), (125000, 16), jnp.float32)
        tbl_20 = 0.05 * jax.random.normal(jax.random.fold_in(_tk, 500 + 20), (1250, 16), jnp.float32)
        tbl_21 = 0.05 * jax.random.normal(jax.random.fold_in(_tk, 500 + 21), (1250, 16), jnp.float32)
        tbl_22 = 0.05 * jax.random.normal(jax.random.fold_in(_tk, 500 + 22), (1250, 16), jnp.float32)
        tbl_23 = 0.05 * jax.random.normal(jax.random.fold_in(_tk, 500 + 23), (1000, 16), jnp.float32)
        tbl_24 = 0.05 * jax.random.normal(jax.random.fold_in(_tk, 500 + 24), (12500, 16), jnp.float32)
        tbl_25 = 0.05 * jax.random.normal(jax.random.fold_in(_tk, 500 + 25), (1000, 16), jnp.float32)
        tbl_26 = 0.05 * jax.random.normal(jax.random.fold_in(_tk, 500 + 26), (1000, 16), jnp.float32)
        tbl_27 = 0.05 * jax.random.normal(jax.random.fold_in(_tk, 500 + 27), (12500, 16), jnp.float32)
        tbl_28 = 0.05 * jax.random.normal(jax.random.fold_in(_tk, 500 + 28), (1250, 16), jnp.float32)
        tbl_29 = 0.05 * jax.random.normal(jax.random.fold_in(_tk, 500 + 29), (1250, 16), jnp.float32)
        tbl_30 = 0.05 * jax.random.normal(jax.random.fold_in(_tk, 500 + 30), (125000, 16), jnp.float32)
        tbl_31 = 0.05 * jax.random.normal(jax.random.fold_in(_tk, 500 + 31), (12500, 16), jnp.float32)
        tbl_32 = 0.05 * jax.random.normal(jax.random.fold_in(_tk, 500 + 32), (1000, 16), jnp.float32)
        tbl_33 = 0.05 * jax.random.normal(jax.random.fold_in(_tk, 500 + 33), (125000, 16), jnp.float32)
        tbl_34 = 0.05 * jax.random.normal(jax.random.fold_in(_tk, 500 + 34), (125000, 16), jnp.float32)
        tbl_35 = 0.05 * jax.random.normal(jax.random.fold_in(_tk, 500 + 35), (12500, 16), jnp.float32)
        tbl_36 = 0.05 * jax.random.normal(jax.random.fold_in(_tk, 500 + 36), (125000, 16), jnp.float32)
        tbl_37 = 0.05 * jax.random.normal(jax.random.fold_in(_tk, 500 + 37), (12500, 16), jnp.float32)
        tbl_38 = 0.05 * jax.random.normal(jax.random.fold_in(_tk, 500 + 38), (12500, 16), jnp.float32)
        _rk = jax.random.fold_in(_tk, 7)
        W_top1 = 0.0693375 * jax.random.normal(jax.random.fold_in(_tk, 801), (208, 512), jnp.float32)
        W_top2 = 0.0441942 * jax.random.normal(jax.random.fold_in(_tk, 802), (512, 256), jnp.float32)
        W_top3 = 0.0625 * jax.random.normal(jax.random.fold_in(_tk, 803), (256, 1), jnp.float32)
        b_top1 = jnp.zeros((512,), jnp.float32)
        b_top2 = jnp.zeros((256,), jnp.float32)
        return (dense_ctx, ids, tbl_0, tbl_1, tbl_2, tbl_3, tbl_4, tbl_5, tbl_6, tbl_7, tbl_8, tbl_9, tbl_10, tbl_11, tbl_12, tbl_13, tbl_14, tbl_15, tbl_16, tbl_17, tbl_18, tbl_19, tbl_20, tbl_21, tbl_22, tbl_23, tbl_24, tbl_25, tbl_26, tbl_27, tbl_28, tbl_29, tbl_30, tbl_31, tbl_32, tbl_33, tbl_34, tbl_35, tbl_36, tbl_37, tbl_38, W_top1, b_top1, W_top2, b_top2, W_top3)
    dense_ctx, ids, tbl_0, tbl_1, tbl_2, tbl_3, tbl_4, tbl_5, tbl_6, tbl_7, tbl_8, tbl_9, tbl_10, tbl_11, tbl_12, tbl_13, tbl_14, tbl_15, tbl_16, tbl_17, tbl_18, tbl_19, tbl_20, tbl_21, tbl_22, tbl_23, tbl_24, tbl_25, tbl_26, tbl_27, tbl_28, tbl_29, tbl_30, tbl_31, tbl_32, tbl_33, tbl_34, tbl_35, tbl_36, tbl_37, tbl_38, W_top1, b_top1, W_top2, b_top2, W_top3 = _rec_inputs()

    def _L0_rec_setup():
        import jax, jax.numpy as jnp
        import numpy as np
        B, F, D = (512, 39, 16)
        L0, L1 = (128, 128)
        H1 = L0 // 2

        def _cin_layer(h, h0, W, b):
            z = jnp.einsum('bhd,bmd->bhmd', h, h0)
            z = z.reshape(z.shape[0], -1, z.shape[-1])
            y = jnp.einsum('oc,bcd->bod', W, z) + b[None, :, None]
            return jax.nn.relu(y)
        key = jax.random.key(seed)
        k0, k1, k2, k3, k4 = jax.random.split(key, 5)
        x = jax.random.normal(k0, (B, F, D), dtype=jnp.float32)
        W0 = jax.random.normal(k1, (L0, F * F), dtype=jnp.float32) * 0.02
        b0 = jnp.zeros((L0,), dtype=jnp.float32)
        W1 = jax.random.normal(k2, (L1, H1 * F), dtype=jnp.float32) * 0.02
        b1 = jnp.zeros((L1,), dtype=jnp.float32)
        return {'x': x, 'W0': W0, 'b0': b0, 'W1': W1, 'b1': b1}
    _L0_rec_all = _L0_rec_setup()
    _L0_rec_in = {k: v for k, v in _L0_rec_all.items() if k in ('W0', 'b0', 'W1', 'b1')}
    del _L0_rec_all
    return {'dense_ctx': dense_ctx, 'ids': ids, 'tbl_0': tbl_0, 'tbl_1': tbl_1, 'tbl_2': tbl_2, 'tbl_3': tbl_3, 'tbl_4': tbl_4, 'tbl_5': tbl_5, 'tbl_6': tbl_6, 'tbl_7': tbl_7, 'tbl_8': tbl_8, 'tbl_9': tbl_9, 'tbl_10': tbl_10, 'tbl_11': tbl_11, 'tbl_12': tbl_12, 'tbl_13': tbl_13, 'tbl_14': tbl_14, 'tbl_15': tbl_15, 'tbl_16': tbl_16, 'tbl_17': tbl_17, 'tbl_18': tbl_18, 'tbl_19': tbl_19, 'tbl_20': tbl_20, 'tbl_21': tbl_21, 'tbl_22': tbl_22, 'tbl_23': tbl_23, 'tbl_24': tbl_24, 'tbl_25': tbl_25, 'tbl_26': tbl_26, 'tbl_27': tbl_27, 'tbl_28': tbl_28, 'tbl_29': tbl_29, 'tbl_30': tbl_30, 'tbl_31': tbl_31, 'tbl_32': tbl_32, 'tbl_33': tbl_33, 'tbl_34': tbl_34, 'tbl_35': tbl_35, 'tbl_36': tbl_36, 'tbl_37': tbl_37, 'tbl_38': tbl_38, 'W_top1': W_top1, 'b_top1': b_top1, 'W_top2': W_top2, 'b_top2': b_top2, 'W_top3': W_top3, 'L0_rec_W0': _L0_rec_in['W0'], 'L0_rec_b0': _L0_rec_in['b0'], 'L0_rec_W1': _L0_rec_in['W1'], 'L0_rec_b1': _L0_rec_in['b1']}

def reference(dense_ctx, ids, tbl_0, tbl_1, tbl_2, tbl_3, tbl_4, tbl_5, tbl_6, tbl_7, tbl_8, tbl_9, tbl_10, tbl_11, tbl_12, tbl_13, tbl_14, tbl_15, tbl_16, tbl_17, tbl_18, tbl_19, tbl_20, tbl_21, tbl_22, tbl_23, tbl_24, tbl_25, tbl_26, tbl_27, tbl_28, tbl_29, tbl_30, tbl_31, tbl_32, tbl_33, tbl_34, tbl_35, tbl_36, tbl_37, tbl_38, W_top1, b_top1, W_top2, b_top2, W_top3, L0_rec_W0, L0_rec_b0, L0_rec_W1, L0_rec_b1):
    import jax
    import jax.numpy as jnp

    def _L0_rec_ref(x, W0, b0, W1, b1):
        import jax, jax.numpy as jnp
        import numpy as np
        B, F, D = (512, 39, 16)
        L0, L1 = (128, 128)
        H1 = L0 // 2

        def _cin_layer(h, h0, W, b):
            z = jnp.einsum('bhd,bmd->bhmd', h, h0)
            z = z.reshape(z.shape[0], -1, z.shape[-1])
            y = jnp.einsum('oc,bcd->bod', W, z) + b[None, :, None]
            return jax.nn.relu(y)
        h0 = x
        y0 = _cin_layer(h0, h0, W0, b0)
        next_hidden, direct0 = (y0[:, :H1, :], y0[:, H1:, :])
        direct1 = _cin_layer(next_hidden, h0, W1, b1)
        result = jnp.sum(jnp.concatenate([direct0, direct1], axis=1), axis=-1)
        return result
    e = jnp.stack([tbl_0[ids[:, 0]], tbl_1[ids[:, 1]], tbl_2[ids[:, 2]], tbl_3[ids[:, 3]], tbl_4[ids[:, 4]], tbl_5[ids[:, 5]], tbl_6[ids[:, 6]], tbl_7[ids[:, 7]], tbl_8[ids[:, 8]], tbl_9[ids[:, 9]], tbl_10[ids[:, 10]], tbl_11[ids[:, 11]], tbl_12[ids[:, 12]], tbl_13[ids[:, 13]], tbl_14[ids[:, 14]], tbl_15[ids[:, 15]], tbl_16[ids[:, 16]], tbl_17[ids[:, 17]], tbl_18[ids[:, 18]], tbl_19[ids[:, 19]], tbl_20[ids[:, 20]], tbl_21[ids[:, 21]], tbl_22[ids[:, 22]], tbl_23[ids[:, 23]], tbl_24[ids[:, 24]], tbl_25[ids[:, 25]], tbl_26[ids[:, 26]], tbl_27[ids[:, 27]], tbl_28[ids[:, 28]], tbl_29[ids[:, 29]], tbl_30[ids[:, 30]], tbl_31[ids[:, 31]], tbl_32[ids[:, 32]], tbl_33[ids[:, 33]], tbl_34[ids[:, 34]], tbl_35[ids[:, 35]], tbl_36[ids[:, 36]], tbl_37[ids[:, 37]], tbl_38[ids[:, 38]]], axis=1)
    z = _L0_rec_ref(e, L0_rec_W0, L0_rec_b0, L0_rec_W1, L0_rec_b1)
    z = z.reshape(z.shape[0], -1)
    h = jnp.concatenate([z, dense_ctx], axis=1)
    h = jnp.maximum(h @ W_top1 + b_top1, 0.0)
    h = jnp.maximum(h @ W_top2 + b_top2, 0.0)
    y = h @ W_top3
    return y

_drawn_inputs = setup_inputs


def setup_inputs(seed=0):
    import zlib

    import numpy as np

    out = dict(_drawn_inputs(seed))
    spreads = {'b_top1': (0.0, 0.8),
     'b_top2': (0.0, 0.35),
     'L0_rec_b0': (0.0, 0.1),
     'L0_rec_b1': (0.0, 0.1)}
    factors = {'tbl_0': 8.0,
     'tbl_1': 8.0,
     'tbl_2': 8.0,
     'tbl_3': 8.0,
     'tbl_4': 8.0,
     'tbl_5': 8.0,
     'tbl_6': 8.0,
     'tbl_7': 8.0,
     'tbl_8': 8.0,
     'tbl_9': 8.0,
     'tbl_10': 8.0,
     'tbl_11': 8.0,
     'tbl_12': 8.0,
     'tbl_13': 8.0,
     'tbl_14': 8.0,
     'tbl_15': 8.0,
     'tbl_16': 8.0,
     'tbl_17': 8.0,
     'tbl_18': 8.0,
     'tbl_19': 8.0,
     'tbl_20': 8.0,
     'tbl_21': 8.0,
     'tbl_22': 8.0,
     'tbl_23': 8.0,
     'tbl_24': 8.0,
     'tbl_25': 8.0,
     'tbl_26': 8.0,
     'tbl_27': 8.0,
     'tbl_28': 8.0,
     'tbl_29': 8.0,
     'tbl_30': 8.0,
     'tbl_31': 8.0,
     'tbl_32': 8.0,
     'tbl_33': 8.0,
     'tbl_34': 8.0,
     'tbl_35': 8.0,
     'tbl_36': 8.0,
     'tbl_37': 8.0,
     'tbl_38': 8.0,
     'L0_rec_W0': 8.0,
     'L0_rec_W1': 3.758}
    for name, (base, spread) in spreads.items():
        noise = np.random.default_rng([zlib.crc32(name.encode()), seed]).standard_normal(out[name].shape)
        drawn = base * np.exp(spread * noise) if base else spread * noise
        out[name] = jnp.asarray(drawn.astype(out[name].dtype))
    for name, factor in factors.items():
        out[name] = (out[name] * factor).astype(out[name].dtype)
    return out
```

```python
from contextlib import ExitStack

import concourse.bass as bass
from concourse import mybir

F32 = mybir.dt.float32
F32R = mybir.dt.float32r
BF16 = mybir.dt.bfloat16
U32 = mybir.dt.uint32
ACT = mybir.ActivationFunctionType
ALU = mybir.AluOpType
AX_X = mybir.AxisListType.X

P = 128
LEAD = 4
RING = 7
NATIVE, BY_DVE, BY_POOL = "native", "low part by VectorE", "low part by GpSimd"


class Group:

    def __init__(self, layer, block, tiles, first, last):
        self.layer, self.block, self.tiles, self.first, self.last = layer, block, tiles, first, last
        self.how = NATIVE
        self.rows = None


def layer_groups(layer, block, tiles):
    pairs = [tiles[t:t + 2] for t in range(0, len(tiles), 2)]
    return [Group(layer, block, p, p is pairs[0], p is pairs[-1]) for p in pairs]


def dlrm_kernel(nc, dense_ctx, ids, tables, W_top1, b_top1, W_top2, b_top2, W_top3, W0, b0, W1, b1, out):
    B, F = ids.shape
    D = tables[0].shape[1]
    L = W0.shape[0]
    H = L // 2
    C = dense_ctx.shape[1]
    M1, M2 = W_top1.shape[1], W_top2.shape[1]
    GROUPS = B // P
    QB = 4
    RB = P // QB
    COLS = RB * D
    GCOLS = QB * COLS
    SHIFTS = F // 2 + 1
    T0 = -(-SHIFTS // 3)
    T1 = -(-F // 2)
    K0 = 3 * F
    K0_LAST = (SHIFTS - 3 * (T0 - 1)) * F
    PARTS = 3
    assert L == P and COLS == 512 and PARTS * F <= P and K0 <= P

    tiles0, tiles1 = list(range(T0)), list(range(T1))
    prologue = layer_groups(0, 0, tiles0) + layer_groups(0, 1, tiles0)

    def body_groups(ends):
        found = []
        for q in range(QB):
            found += layer_groups(1, q, tiles1)
            if not (ends and q + 2 >= QB):
                found += layer_groups(0, q + 2, tiles0)
        return found

    loop_body, last_body = body_groups(False), body_groups(True)
    PRO, BODY = len(prologue), len(loop_body)
    assert BODY % RING == 0 and BODY % 2 == 0 and PRO % 2 == 0

    POOL_FROM = 26
    for k, g in enumerate(prologue):
        g.how = NATIVE if g.last else BY_DVE
    for body in (loop_body, last_body):
        for k, g in enumerate(body):
            if k < POOL_FROM and body is loop_body:
                g.how = NATIVE if (g.last or k % 5 in (1, 3)) else BY_DVE
            else:
                g.how = BY_POOL if k % 4 in (0, 2, 3) else BY_DVE
                if g.last and g.layer == 0:
                    g.how = NATIVE
                if k % 14 == 6:
                    g.how = BY_DVE

    def count_before(groups, k, how):
        return sum(g.how == how for g in groups[:k])

    with ExitStack() as ctx:
        def sb(name, shape, dt=F32):
            return ctx.enter_context(nc.sbuf_tensor(name, shape, dt))

        def sem(name):
            return ctx.enter_context(nc.semaphore(name))

        bank = [ctx.enter_context(nc.psum_tensor(f"bank{n}", [P, 1024], F32)) for n in range(4)]
        spread = bank[0:2]
        acc = {0: bank[2][:, 0:512], 1: bank[2][:, 512:1024]}
        misc = [bank[3][:, 0:512], bank[3][:, 512:1024]]

        idx = sb("idx", [P, F], mybir.dt.int32)
        gathered = sb("gathered", [P, F, D])
        e_dmajor = sb("e_dmajor", [P, D, 3, F])
        e_rest = sb("e_rest", [P, D, F])
        e_parts = sb("e_parts", [P, D, P], BF16)
        e_copies = sb("e_copies", [P, 2 * GCOLS])
        e_stack = sb("e_stack", [P, 2 * GCOLS], BF16)
        hidden = sb("hidden", [P, 2, COLS])
        relu0 = sb("relu0", [H, 2, COLS])
        relu1 = sb("relu1", [P, 2, COLS])
        z = sb("z", [P, RING, 2, COLS])
        z_high = sb("z_high", [P, RING, 2, COLS], F32R)
        z_low = sb("z_low", [P, RING, 2, COLS], F32R)

        WIDE = F + SHIFTS - 1
        z_flat = z[:].rearrange("p r t c -> p (r t c)")
        at = [0]
        for size in (F * F, F * WIDE, SHIFTS * F, H * F):
            at.append(at[-1] + size)
        w0_in = z_flat[:, at[0]:at[1]].rearrange("p (h m) -> p h m", h=F)
        w0_sym = z_flat[:, at[1]:at[2]]
        w0_rows = z_flat[:, at[2]:at[3]]
        w1_rows = z_flat[:, at[3]:at[4]]
        w1_in = e_copies[:, 0:H * F].rearrange("p (h m) -> p h m", h=H)
        w_full = sb("w_full", [P, T0 + T1, L])
        w_high = sb("w_high", [P, T0 + T1, L], F32R)
        w_low = sb("w_low", [P, T0 + T1, L], F32R)
        ident = sb("ident", [P, P])
        ident_bf = sb("ident_bf", [P, P], BF16)
        pick = sb("pick", [P, F + 1], BF16)
        pick_wide = sb("pick_wide", [P, F + 3 * T0 - 1], BF16)
        pick0 = sb("pick0", [P, T0, 3, F], BF16)
        pick1 = sb("pick1", [P, T1, 2, H], BF16)
        bias0, bias1 = sb("bias0", [P, 1]), sb("bias1", [P, 1])

        top_a = sb("top_a", [H + C, B])
        top_b = sb("top_b", [P, B])
        dense = sb("dense", [P, GROUPS, H + C])
        wt1_a, wt1_b = sb("wt1_a", [H + C, M1]), sb("wt1_b", [P, M1])
        wt2 = sb("wt2", [P, M1 // P, M2])
        wt3 = sb("wt3", [P, M2 // P])
        bias_t1, bias_t2 = sb("bias_t1", [P, M1 // P]), sb("bias_t2", [P, M2 // P])
        N = B // 2

        def mlp_h1(half_, t):
            c = (half_ * (M1 // P) + t) * N
            return z_flat[:, c:c + N]

        def mlp_h2(half_, t):
            c = (2 * (M1 // P) + half_ * (M2 // P) + t) * N
            return z_flat[:, c:c + N]

        y_row = sb("y_row", [1, B])

        s_idx, s_w0, s_w1, s_small, s_top = map(sem, ("s_idx", "s_w0", "s_w1", "s_small", "s_top"))
        s_gather = sem("s_gather")
        s_gather_go = sem("s_gather_go")
        s_const = sem("s_const")
        s_zeroed = sem("s_zeroed")
        s_sym = sem("s_sym")
        s_pick = sem("s_pick")
        s_w1_rows = sem("s_w1_rows")
        s_wt = sem("s_wt")
        s_wt_high, s_wt_low = sem("s_wt_high"), sem("s_wt_low")
        s_dense_t, s_dense = sem("s_dense_t"), sem("s_dense")
        s_eprep_act, s_eprep_dve = sem("s_eprep_act"), sem("s_eprep_dve")
        s_etr = sem("s_etr")
        s_eout = sem("s_eout")
        s_spread = sem("s_spread")
        s_z = sem("s_z")
        s_high = sem("s_high")
        s_low_dve, s_low_pool = sem("s_low_dve"), sem("s_low_pool")
        s_main = sem("s_main")
        s_read0, s_read1 = sem("s_read0"), sem("s_read1")
        s_hid = sem("s_hid")
        s_sum0, s_sum1 = sem("s_sum0"), sem("s_sum1")
        s_mlp, s_mlp_act, s_out = sem("s_mlp"), sem("s_mlp_act"), sem("s_out")

        E_BANKS = 6
        E_STEP = 27
        E_FILL = {27: (0, 1), 28: (2, 3), 29: (4, 5)}
        E_OUT = {30: (0, 1), 31: (2, 3), 32: (4, 5)}

        WBANKS = [(0, 4, [(K0, 0, 4)]), (4, 3, [(K0, 0, 2), (K0_LAST, 2, 1)])]
        WBANKS += [(T0 + 4 * n, 4, [(P, 0, 4)]) for n in range(T1 // 4 - 1)]
        WBANKS += [(T0 + T1 - 4, 4, [(P, 0, 3), (H, 3, 1)])]

        def wbank(n):
            return spread[n % 4 // 2][:, n % 2 * 512:n % 2 * 512 + 512].rearrange("p (t o) -> p t o", o=L)

        def mlp_bank(n):
            return bank[n // 2][:, n % 2 * 512:n % 2 * 512 + 512]

        HIGH_PRO, HIGH_BODY = (sum(g.how != NATIVE for g in x) for x in (prologue, loop_body))

        def high_count(i, groups, k):
            start = 0 if groups is prologue else HIGH_PRO + HIGH_BODY * i
            return start + sum(g.how != NATIVE for g in groups[:k + 1])

        def low_count(i, groups, k):
            how = groups[k].how
            start = 0 if groups is prologue else \
                count_before(prologue, PRO, how) + count_before(loop_body, BODY, how) * i
            return start + count_before(groups, k + 1, how)

        def group_count(i, groups, k):
            return k if groups is prologue else PRO + BODY * i + k

        def ring_of(groups, k):
            return (k if groups is prologue else PRO + k) % RING

        def rows_of(g):
            return K0 if g.layer == 0 else P

        def weight_tile(g, t):
            return t if g.layer == 0 else T0 + t

        def product_rows(g, t):
            return K0_LAST if (g.layer, t) == (0, T0 - 1) else rows_of(g)

        def half(i, g):
            return ((i + g.block // QB) % 2) * GCOLS + (g.block % QB) * COLS

        ids_v = ids.rearrange("(g p) f -> g p f", p=P)
        block = ctx.enter_context(nc.Block())

        @block.sync
        def _(sp):
            sp.dma_start(idx[:], ids_v[0]).then_inc(s_idx, 16)
            w0_v = W0.rearrange("o (h m) -> o h m", h=F)
            sp.dma_start(w0_in[0:H], w0_v[H:L]).then_inc(s_w0, 16)
            sp.dma_start(w0_in[H:L], w0_v[0:H]).then_inc(s_w0, 16)
            sp.dma_start(w1_in, W1.rearrange("o (h m) -> o h m", h=H)).then_inc(s_w1, 16)
            b0_v = b0.rearrange("(p a) -> p a", a=1)
            sp.dma_start(bias0[0:H], b0_v[H:L]).then_inc(s_small, 16)
            sp.dma_start(bias0[H:L], b0_v[0:H]).then_inc(s_small, 16)
            sp.dma_start(bias1[:], b1.rearrange("(p a) -> p a", a=1)).then_inc(s_small, 16)
            sp.wait_ge(s_zeroed, 2)
            sp.dma_start(dense[:, :, H:H + C], dense_ctx.rearrange("(g p) c -> p g c", p=P)).then_inc(s_top, 16)
            sp.dma_start(wt1_a[0:H], W_top1[0:H]).then_inc(s_top, 16)
            sp.dma_start(wt1_a[H:H + C], W_top1[H + L:H + L + C]).then_inc(s_top, 16)
            sp.dma_start(wt1_b[:], W_top1[H:H + L]).then_inc(s_top, 16)
            sp.dma_start(wt2[:], W_top2.rearrange("(p t) n -> p t n", p=P)).then_inc(s_top, 16)
            sp.dma_start(wt3[:], W_top3.rearrange("(p t) n -> p (t n)", p=P)).then_inc(s_top, 16)
            sp.dma_start(bias_t1[:], b_top1.rearrange("(p t) -> p t", p=P)).then_inc(s_top, 16)
            sp.dma_start(bias_t2[:], b_top2.rearrange("(p t) -> p t", p=P)).then_inc(s_top, 16)
            with sp.Fori(0, GROUPS - 1) as i:
                sp.wait_ge(s_gather, (i + 1) * (16 * F))
                sp.dma_start(idx[:], ids_v[bass.ds(i + 1, 1)].rearrange("g p f -> p (g f)")).then_inc(s_idx, 16)
            sp.wait_ge(s_mlp_act, 14)
            sp.dma_start(out.rearrange("b a -> a b"), y_row[:]).then_inc(s_out, 16)
            sp.wait_ge(s_out, 16)

        @block.gpsimd
        def _(pool):
            for tile in (ident, ident_bf, pick):
                pool.memset(tile[:], 0.0).then_inc(s_const, 1)
            pool.wait_ge(s_const, 3)
            for tile in (ident, ident_bf):
                pool.affine_select(out=tile[:], in_=tile[:], compare_op=ALU.not_equal, fill=1.0, base=0,
                                   pattern=[[-1, P]], channel_multiplier=1).then_inc(s_const, 1)
            for part in range(PARTS):
                pool.wait_ge(s_const, 5 + part)
                pool.affine_select(out=pick[:, 0:F + 1], in_=pick[:, 0:F + 1], compare_op=ALU.not_equal,
                                   fill=1.0, base=-part, pattern=[[-PARTS, F + 1]],
                                   channel_multiplier=1).then_inc(s_const, 1)

            def gather(f):
                pool.indirect_dma_start(gathered[:, f, :], None, tables[f],
                                        bass.IndirectOffsetOnAxis(idx[:, f:f + 1].bitcast(U32), 0)
                                        ).then_inc(s_gather, 16)

            def low_part(i, groups, k):
                g = groups[k]
                r, n, rows = ring_of(groups, k), len(g.tiles), rows_of(g)
                pool.wait_ge(s_high, high_count(i, groups, k))
                pool.tensor_tensor(z_low[0:rows, r, 0:n], z[0:rows, r, 0:n],
                                   z_high[0:rows, r, 0:n].bitcast(F32), ALU.subtract).then_inc(s_low_pool, 1)

            pool.wait_ge(s_idx, 16)
            for f in range(F):
                gather(f)

            def body(i, groups, gathers):
                if gathers:
                    pool.wait_ge(s_idx, 16 * (i + 2))
                    pool.wait_ge(s_eprep_act, 3 * (i + 1))
                    pool.sem_inc(s_gather_go, 1)
                    for f in range(F):
                        gather(f)
                for k, g in enumerate(groups):
                    if g.how == BY_POOL:
                        low_part(i, groups, k)

            with pool.Fori(0, GROUPS - 1) as i:
                body(i, loop_body, True)
            body(GROUPS - 1, last_body, False)

        @block.scalar
        def _(act):
            def e_split(i, step):
                part = lambda n: e_parts[:, :, 0:PARTS * F].rearrange("p d (f n) -> p d f n", n=PARTS)[:, :, :, n]
                if step == 0:
                    act.wait_ge(s_gather, (16 * F) * (i + 1))
                    act.activation(e_dmajor[:], gathered[:].rearrange("p f (d o) -> p d o f", o=1)
                                   .broadcast_to([P, D, 3, F]), ACT.Copy).then_inc(s_eprep_act, 1)
                    act.activation(part(0), gathered[:].rearrange("p f d -> p d f"), ACT.Copy).then_inc(s_eprep_act, 1)
                else:
                    act.wait_ge(s_eprep_dve, 2 * i + 1)
                    act.activation(part(1), e_rest[:], ACT.Copy).then_inc(s_eprep_act, 1)

            def e_out(i, n):
                act.wait_ge(s_etr, E_BANKS * i + n + 1)
                dims, src = (4, misc[n % 2][0:K0]) if n < 4 else (8, misc[n % 2].bitcast(BF16))
                d0 = dims * (n if n < 4 else n - 4)
                rows, to = (K0, e_copies) if n < 4 else (P, e_stack)
                dst = to[0:rows, bass.ds((i % 2) * GCOLS, GCOLS)] if not isinstance(i, int) else \
                    to[0:rows, (i % 2) * GCOLS:(i % 2 + 1) * GCOLS]
                act.activation(dst.rearrange("p (q d b) -> p d q b", q=QB, d=D)[:, d0:d0 + dims],
                               src.rearrange("p (d q b) -> p d q b", d=dims, q=QB), ACT.Copy).then_inc(s_eout, 1)

            def high_part(i, groups, k):
                g = groups[k]
                if g.how == NATIVE:
                    return
                r, n, rows = ring_of(groups, k), len(g.tiles), rows_of(g)
                act.wait_ge(s_z, group_count(i, groups, k) + 1)
                act.activation(z_high[0:rows, r, 0:n], z[0:rows, r, 0:n], ACT.Copy).then_inc(s_high, 1)

            def read_sums0(c_even, done):
                b = c_even
                act.wait_ge(s_main, done)
                act.activation(hidden[H:L, b], acc[0][H:L], ACT.Relu, bias=bias0[H:L]).then_inc(s_read0, 1)
                act.activation(relu0[:, b], acc[0][0:H], ACT.Relu, bias=bias0[0:H]).then_inc(s_read0, 1)

            def copy_hidden(b, done):
                act.wait_ge(s_read0, done)
                act.activation(hidden[0:H, b], hidden[H:L, b], ACT.Copy).then_inc(s_hid, 1)

            def read_sums1(b, done):
                act.wait_ge(s_main, done)
                act.activation(relu1[:, b], acc[1], ACT.Relu, bias=bias1[:]).then_inc(s_read1, 1)

            act.wait_ge(s_w1, 16)
            act.activation(w1_rows.rearrange("p (m h) -> p m h", h=H), w1_in.rearrange("p h m -> p m h"),
                           ACT.Copy).then_inc(s_w1_rows, 1)
            act.wait_ge(s_zeroed, 5)
            for n, (w, cnt, rows) in enumerate(WBANKS):
                act.wait_ge(s_wt, n + 1)
                for rr, c0, cc in rows:
                    ins = act.activation(w_high[0:rr, w + c0:w + c0 + cc], wbank(n)[0:rr, c0:c0 + cc], ACT.Copy)
                ins.then_inc(s_wt_high, 1)
            act.wait_ge(s_small, 48)
            act.nop().then_inc(s_read1, 1)
            e_split(0, 0)
            e_split(0, 1)
            for n in range(E_BANKS):
                e_out(0, n)
            act.wait_ge(s_dense_t, 1)
            dv = top_a[H:H + C].rearrange("c (x b) -> c x b", x=2)
            act.activation(dv[:, 0], misc[0][H:H + C], ACT.Copy).then_inc(s_dense, 1)
            act.activation(dv[:, 1], misc[1][H:H + C], ACT.Copy).then_inc(s_dense, 1)

            after = LEAD - 1
            for k, g in enumerate(prologue):
                high_part(0, prologue, k)
                if k - after >= 0 and prologue[k - after].last:
                    read_sums0(0, k - after + 1)
                    copy_hidden(0, 1)

            def body(i, groups):
                for k, g in enumerate(groups):
                    high_part(i, groups, k)
                    if k == after - 1:
                        read_sums0(1, group_count(i, groups, 0))
                        copy_hidden(1, 2 * (i * QB + 2) - 1)
                    j = k - after
                    if j >= 0 and groups[j].last:
                        done = group_count(i, groups, j) + 1
                        if groups[j].layer == 1:
                            read_sums1(groups[j].block % 2, done)
                        else:
                            c = groups[j].block
                            read_sums0(c % 2, done)
                            copy_hidden(c % 2, 2 * (i * QB + c + 1) - 1)
                    if groups is loop_body:
                        if k == E_STEP:
                            e_split(i + 1, 0)
                        if k == E_STEP + 2:
                            e_split(i + 1, 1)
                        if k in E_OUT:
                            for n in E_OUT[k]:
                                e_out(i + 1, n)

            with act.Fori(0, GROUPS - 1) as i:
                body(i, loop_body)
            body(GROUPS - 1, last_body)
            read_sums1(1, group_count(GROUPS - 1, last_body, len(last_body)))

            for n in range(M1 // P * 2):
                hf, t = divmod(n, M1 // P)
                act.wait_ge(s_mlp, n + 1)
                act.activation(mlp_h1(hf, t), mlp_bank(n), ACT.Relu, bias=bias_t1[:, t:t + 1]).then_inc(s_mlp_act, 1)
            for n in range(M2 // P * 2):
                hf, t = divmod(n, M2 // P)
                act.wait_ge(s_mlp, 8 + n + 1)
                act.activation(mlp_h2(hf, t), mlp_bank(n), ACT.Relu, bias=bias_t2[:, t:t + 1]).then_inc(s_mlp_act, 1)
            for hf in range(2):
                act.wait_ge(s_mlp, 12 + hf + 1)
                act.activation(y_row[0:1, hf * 512:(hf + 1) * 512], mlp_bank(4 + hf)[0:1], ACT.Copy).then_inc(s_mlp_act, 1)

        @block.vector
        def _(dve):
            dve.memset(e_parts[:], 0.0).then_inc(s_zeroed, 1)
            dve.memset(dense[:], 0.0).then_inc(s_zeroed, 1)
            for w in (w_full, w_high, w_low):
                dve.memset(w[:, T0 + T1 - 1].bitcast(F32), 0.0).then_inc(s_zeroed, 1)
            dve.wait_ge(s_w0, 32)
            sym = w0_sym.rearrange("p (h m) -> p h m", m=WIDE)
            dve.tensor_tensor(sym[:, :, 0:F], w0_in, w0_in.rearrange("p h m -> p m h"), ALU.add).then_inc(s_sym, 1)
            diagonal = w0_sym[:, 0:(WIDE + 1) * (F - 1) + 1:WIDE + 1]
            dve.wait_ge(s_sym, 1)
            dve.tensor_scalar(diagonal, diagonal, 0.5, None, ALU.mult).then_inc(s_sym, 1)
            dve.wait_ge(s_sym, 2)
            dve.tensor_copy(sym[:, :, F:WIDE], sym[:, :, 0:WIDE - F]).then_inc(s_sym, 1)
            dve.wait_ge(s_sym, 3)
            windows = bass.AP(w0_sym.tensor, w0_sym.offset, [w0_sym.ap[0], [1, SHIFTS], [WIDE + 1, F]])
            dve.tensor_copy(w0_rows.rearrange("p (s h) -> p s h", h=F), windows).then_inc(s_sym, 1)
            dve.wait_ge(s_const, 5 + PARTS)
            dve.tensor_copy(pick1[:], pick[:, 0:F + 1].rearrange("p (t j o) -> p t j o", j=2, o=1)
                            .broadcast_to([P, T1, 2, H])).then_inc(s_pick, 1)
            dve.tensor_copy(pick_wide[:, 0:F], pick[:, 0:F]).then_inc(s_pick, 1)
            dve.tensor_copy(pick_wide[:, F:], pick[:, 0:3 * T0 - 1]).then_inc(s_pick, 1)
            dve.wait_ge(s_pick, 3)
            wide = pick_wide[:]
            windows = bass.AP(wide.tensor, wide.offset, [wide.ap[0], [3, T0], [1, 3], [1, F]])
            dve.tensor_copy(pick0[:], windows).then_inc(s_pick, 1)
            dve.wait_ge(s_zeroed, 5)
            for n, (w, cnt, rows) in enumerate(WBANKS):
                dve.wait_ge(s_wt_high, n + 1)
                for rr, c0, cc in rows:
                    dve.tensor_copy(w_full[0:rr, w + c0:w + c0 + cc], wbank(n)[0:rr, c0:c0 + cc])
                    ins = dve.tensor_tensor(w_low[0:rr, w + c0:w + c0 + cc], wbank(n)[0:rr, c0:c0 + cc],
                                            w_high[0:rr, w + c0:w + c0 + cc].bitcast(F32), ALU.subtract)
                ins.then_inc(s_wt_low, 1)

            def e_rest_of(i, step):
                part = lambda n: e_parts[:, :, 0:PARTS * F].rearrange("p d (f n) -> p d f n", n=PARTS)[:, :, :, n]
                if step == 0:
                    dve.wait_ge(s_eprep_act, 3 * i + 2)
                    dve.tensor_tensor(e_rest[:], e_dmajor[:, :, 0], part(0), ALU.subtract).then_inc(s_eprep_dve, 1)
                else:
                    dve.wait_ge(s_eprep_act, 3 * i + 3)
                    dve.tensor_tensor(part(2), e_rest[:], part(1), ALU.subtract).then_inc(s_eprep_dve, 1)

            def form_z(i, groups, k):
                g = groups[k]
                r, n, rows = ring_of(groups, k), len(g.tiles), rows_of(g)
                if not (groups is prologue and k < RING):
                    dve.wait_ge(s_main, group_count(i, groups, k) - RING + 1)
                if g.layer == 1 and g.first:
                    dve.wait_ge(s_hid, i * QB + g.block + 1)
                dve.wait_ge(s_spread, group_count(i, groups, k) + 1)
                if g.layer == 1:
                    kept = hidden[:, g.block % 2]
                else:
                    start = half(i, g)
                    kept = e_copies[0:rows, start:start + COLS] if isinstance(start, int) else \
                        e_copies[0:rows, bass.ds(start, COLS)]
                kept = kept.rearrange("p (o c) -> p o c", o=1).broadcast_to([rows, n, COLS])
                other = spread[k % 2][0:rows, 0:n * COLS].rearrange("p (t c) -> p t c", t=n)
                dve.tensor_tensor(z[0:rows, r, 0:n], other, kept, ALU.mult).then_inc(s_z, 1)

            def low_part(i, groups, k):
                g = groups[k]
                if g.how != BY_DVE:
                    return
                r, n, rows = ring_of(groups, k), len(g.tiles), rows_of(g)
                dve.wait_ge(s_high, high_count(i, groups, k))
                dve.tensor_tensor(z_low[0:rows, r, 0:n], z[0:rows, r, 0:n],
                                  z_high[0:rows, r, 0:n].bitcast(F32), ALU.subtract).then_inc(s_low_dve, 1)

            def sum_dims(layer, b, done, column):
                src, rows, to = (relu0, H, top_a) if layer == 0 else (relu1, P, top_b)
                dve.wait_ge(s_read0 if layer == 0 else s_read1, done)
                dst = to[0:rows, column:column + RB] if isinstance(column, int) else to[0:rows, bass.ds(column, RB)]
                dve.tensor_reduce(dst, src[:, b].rearrange("p (d b) -> p b d", d=D), AX_X, ALU.add) \
                   .then_inc(s_sum0 if layer == 0 else s_sum1, 1)

            e_rest_of(0, 0)
            e_rest_of(0, 1)
            for k in range(PRO):
                form_z(0, prologue, k)
                if k:
                    low_part(0, prologue, k - 1)
            after = LEAD

            def body(i, groups):
                for k, g in enumerate(groups):
                    form_z(i, groups, k)
                    if k:
                        low_part(i, groups, k - 1)
                    if k == after:
                        sum_dims(0, 1, 2 * (i * QB + 2), i * P + RB)
                    if k == after + 1:
                        sum_dims(0, 0, 2 * (i * QB + 1), i * P)
                    j = k - after
                    if j >= 0 and groups[j].last:
                        c = groups[j].block
                        if groups[j].layer == 1:
                            sum_dims(1, c % 2, i * QB + c + 2, i * P + c * RB)
                        elif c < QB:
                            sum_dims(0, c % 2, 2 * (i * QB + c + 1), i * P + c * RB)
                    if groups is loop_body:
                        if k == E_STEP + 1:
                            e_rest_of(i + 1, 0)
                        if k == E_STEP + 3:
                            e_rest_of(i + 1, 1)
                low_part(i, groups, len(groups) - 1)

            with dve.Fori(0, GROUPS - 1) as i:
                body(i, loop_body)
            body(GROUPS - 1, last_body)
            c = GROUPS * QB - 1
            sum_dims(1, 1, c + 2, c * RB)

        @block.tensor
        def _(pe):
            pe.wait_ge(s_const, 5)
            pe.wait_ge(s_sym, 4)
            for n, (w, cnt, rows) in enumerate(WBANKS):
                if n == 2:
                    pe.wait_ge(s_w1_rows, 1)
                if n >= 4:
                    pe.wait_ge(s_wt_low, n - 3)
                for t in range(cnt):
                    if w < T0:
                        c, size = (w + t) * K0, K0 if w + t < T0 - 1 else K0_LAST
                        src = w0_rows[:, c:c + size]
                    else:
                        c = (w - T0 + t) * P
                        size = min(P, H * F - c)
                        src = w1_rows[:, c:c + size]
                    ins = pe.transpose(wbank(n)[0:size, t], src, ident[:])
                ins.then_inc(s_wt, 1)

            def e_transpose(i, n):
                if not (isinstance(i, int) and i == 0 and n < 2):
                    pe.wait_ge(s_eout, E_BANKS * i + n - 1)
                if n < 4:
                    pe.wait_ge(s_eprep_act, 3 * i + 1)
                    for d in range(4):
                        src = e_dmajor[:, 4 * n + d].rearrange("p o f -> p (o f)")
                        ins = pe.transpose(misc[n % 2][0:K0, d * P:(d + 1) * P], src, ident[:])
                else:
                    pe.wait_ge(s_eprep_dve, 2 * i + 2)
                    bank16 = misc[n % 2].bitcast(BF16)
                    for d in range(8):
                        ins = pe.transpose(bank16[:, d * P:(d + 1) * P], e_parts[:, 8 * (n - 4) + d], ident_bf[:])
                ins.then_inc(s_etr, 1)

            def spread_group(i, groups, k):
                g = groups[k]
                if not (groups is prologue and k < 2):
                    pe.wait_ge(s_z, group_count(i, groups, k) - 1)
                if g.layer == 0 and g.first and (g.block % QB == 0):
                    pe.wait_ge(s_eout, E_BANKS * (i + g.block // QB + 1))
                start = half(i, g)
                moving = e_stack[:, start:start + COLS] if isinstance(start, int) else e_stack[:, bass.ds(start, COLS)]
                for x, t in enumerate(g.tiles):
                    picks = pick0[:, t].rearrange("p j h -> p (j h)") if g.layer == 0 else \
                        pick1[:, t].rearrange("p j h -> p (j h)")
                    ins = pe.matmul(spread[k % 2][0:rows_of(g), x * COLS:(x + 1) * COLS], picks, moving,
                                    start=True, stop=True)
                ins.then_inc(s_spread, 1)

            def multiply(i, groups, k):
                g = groups[k]
                r = ring_of(groups, k)
                if g.first and not (groups is prologue and k == 0):
                    c = i * QB + g.block
                    if g.layer == 0:
                        pe.wait_ge(s_read0, 2 * c)
                    else:
                        pe.wait_ge(s_read1, c + 1)
                passes = [(w_full, z, s_z, group_count(i, groups, k) + 1)]
                if g.how != NATIVE:
                    low = s_low_dve if g.how == BY_DVE else s_low_pool
                    passes = [(w_high, z_high, s_high, high_count(i, groups, k)),
                              (w_low, z_high, None, None),
                              (w_high, z_low, low, low_count(i, groups, k))]
                for n, (w, moving, ready, value) in enumerate(passes):
                    if ready is not None:
                        pe.wait_ge(ready, value)
                    for x, t in enumerate(g.tiles):
                        kk = product_rows(g, t)
                        ins = pe.matmul(acc[g.layer], w[0:kk, weight_tile(g, t)], moving[0:kk, r, x],
                                        start=g.first and n == 0 and x == 0,
                                        stop=g.last and n == len(passes) - 1 and x == len(g.tiles) - 1)
                ins.then_inc(s_main, 1)

            for n in range(E_BANKS):
                e_transpose(0, n)
            pe.wait_ge(s_top, 128)
            pe.wait_ge(s_eout, E_BANKS)
            for gi in range(GROUPS):
                ins = pe.transpose(misc[gi // 4][0:H + C, (gi % 4) * P:(gi % 4 + 1) * P], dense[:, gi], ident[:])
            ins.then_inc(s_dense_t, 1)
            pe.wait_ge(s_wt_low, len(WBANKS))
            pe.wait_ge(s_pick, 4)

            for k in range(LEAD):
                spread_group(0, prologue, k)
            for k in range(PRO):
                if k + LEAD < PRO:
                    spread_group(0, prologue, k + LEAD)
                else:
                    spread_group(0, loop_body, k + LEAD - PRO)
                multiply(0, prologue, k)

            def body(i, groups):
                for k in range(len(groups)):
                    if k + LEAD < len(groups):
                        spread_group(i, groups, k + LEAD)
                    elif groups is loop_body:
                        spread_group(i + 1, loop_body, k + LEAD - BODY)
                    multiply(i, groups, k)
                    if groups is loop_body and k in E_FILL:
                        for n in E_FILL[k]:
                            e_transpose(i + 1, n)

            with pe.Fori(0, GROUPS - 1) as i:
                body(i, loop_body)
            body(GROUPS - 1, last_body)

            for hf in range(2):
                if hf == 0:
                    pe.wait_ge(s_dense, 2)
                    pe.wait_ge(s_read1, GROUPS * QB + 1)
                pe.wait_ge(s_sum1, (hf + 1) * GROUPS * QB // 2)
                pe.wait_ge(s_sum0, (hf + 1) * GROUPS * QB // 2)
                for t in range(M1 // P):
                    o = mlp_bank(hf * (M1 // P) + t)
                    pe.matmul(o, wt1_a[:, t::M1 // P], top_a[:, hf * N:(hf + 1) * N], start=True, stop=False)
                    pe.matmul(o, wt1_b[:, t::M1 // P], top_b[:, hf * N:(hf + 1) * N],
                              start=False, stop=True).then_inc(s_mlp, 1)
            for hf in range(2):
                for t in range(M2 // P):
                    for kt in range(M1 // P):
                        if t == 0:
                            pe.wait_ge(s_mlp_act, hf * (M1 // P) + kt + 1)
                        ins = pe.matmul(mlp_bank(hf * (M2 // P) + t), wt2[:, kt, t::M2 // P], mlp_h1(hf, kt),
                                        start=kt == 0, stop=kt == M1 // P - 1)
                    ins.then_inc(s_mlp, 1)
            for hf in range(2):
                for kt in range(M2 // P):
                    pe.wait_ge(s_mlp_act, 8 + hf * (M2 // P) + kt + 1)
                    ins = pe.matmul(mlp_bank(4 + hf)[0:1], wt3[:, kt:kt + 1], mlp_h2(hf, kt),
                                    start=kt == 0, stop=kt == M2 // P - 1)
                ins.then_inc(s_mlp, 1)


def kernel(**inputs):
    import numpy as np
    import concourse.bacc as bacc
    from concourse.bass_utils import run_bass_kernel_spmd

    nc = bacc.Bacc("TRN2", target_bir_lowering=False, num_devices=1)
    arrays, aps = {}, {}
    for name, value in inputs.items():
        a = np.ascontiguousarray(value)
        arrays[f"in_{name}"] = a
        aps[name] = nc.dram_tensor(f"in_{name}", a.shape, mybir.dt.from_np(a.dtype), kind="ExternalInput").ap()
    rows, fields = inputs["ids"].shape
    out = nc.dram_tensor("out_y", (rows, 1), F32, kind="ExternalOutput").ap()
    dlrm_kernel(nc, aps["dense_ctx"], aps["ids"], [aps[f"tbl_{f}"] for f in range(fields)],
                aps["W_top1"], aps["b_top1"], aps["W_top2"], aps["b_top2"], aps["W_top3"],
                aps["L0_rec_W0"], aps["L0_rec_b0"], aps["L0_rec_W1"], aps["L0_rec_b1"], out)
    r = run_bass_kernel_spmd(nc, [arrays], core_ids=[0])
    return r.results[0]["out_y"]
```

```python
from contextlib import ExitStack

import concourse.bass as bass
from concourse import mybir

F32 = mybir.dt.float32
F32R = mybir.dt.float32r
BF16 = mybir.dt.bfloat16
U32 = mybir.dt.uint32
ACT = mybir.ActivationFunctionType
ALU = mybir.AluOpType
AX_X = mybir.AxisListType.X

P = 128
LEAD = 4
RING = 7
NATIVE, BY_DVE, BY_POOL = "native", "low part by VectorE", "low part by GpSimd"


PROLOGUE_HOW = "DDDN DDDN"
LOOP_HOW = ("DNDDNDNDND DNDN"
            "NDNDNDPDPP DPDN"
            "PDPPDPDPPD PDPN"
            "PDPPDPDPDN DNDN")
LAST_HOW = ("PDPPDPDPPD PDPN"
            "PDPPDPDPPD PDPN"
            "PDPPDPDPPD"
            "PDPPDPDPPD")


class Group:

    def __init__(self, layer, block, tiles, first, last):
        self.layer, self.block, self.tiles, self.first, self.last = layer, block, tiles, first, last
        self.how = NATIVE
        self.rows = None


def layer_groups(layer, block, tiles):
    pairs = [tiles[t:t + 2] for t in range(0, len(tiles), 2)]
    return [Group(layer, block, p, p is pairs[0], p is pairs[-1]) for p in pairs]


def dlrm_kernel(nc, dense_ctx, ids, tables, W_top1, b_top1, W_top2, b_top2, W_top3, W0, b0, W1, b1, out):
    B, F = ids.shape
    D = tables[0].shape[1]
    L = W0.shape[0]
    H = L // 2
    C = dense_ctx.shape[1]
    M1, M2 = W_top1.shape[1], W_top2.shape[1]
    GROUPS = B // P
    QB = 4
    RB = P // QB
    COLS = RB * D
    GCOLS = QB * COLS
    SHIFTS = F // 2 + 1
    T0 = -(-SHIFTS // 3)
    T1 = -(-F // 2)
    K0 = 3 * F
    K0_LAST = (SHIFTS - 3 * (T0 - 1)) * F
    PARTS = 3
    assert L == P and COLS == 512 and PARTS * F <= P and K0 <= P

    tiles0, tiles1 = list(range(T0)), list(range(T1))
    prologue = layer_groups(0, 0, tiles0) + layer_groups(0, 1, tiles0)

    def body_groups(ends):
        found = []
        for q in range(QB):
            found += layer_groups(1, q, tiles1)
            if not (ends and q + 2 >= QB):
                found += layer_groups(0, q + 2, tiles0)
        return found

    loop_body, last_body = body_groups(False), body_groups(True)
    PRO, BODY = len(prologue), len(loop_body)
    assert BODY % RING == 0 and BODY % 2 == 0 and PRO % 2 == 0

    HOW = {"N": NATIVE, "D": BY_DVE, "P": BY_POOL}
    for groups, letters in ((prologue, PROLOGUE_HOW), (loop_body, LOOP_HOW), (last_body, LAST_HOW)):
        letters = letters.replace(" ", "")
        assert len(letters) == len(groups)
        for g, letter in zip(groups, letters):
            g.how = HOW[letter]

    def count_before(groups, k, how):
        return sum(g.how == how for g in groups[:k])

    with ExitStack() as ctx:
        def sb(name, shape, dt=F32):
            return ctx.enter_context(nc.sbuf_tensor(name, shape, dt))

        def sem(name):
            return ctx.enter_context(nc.semaphore(name))

        bank = [ctx.enter_context(nc.psum_tensor(f"bank{n}", [P, 1024], F32)) for n in range(4)]
        spread = bank[0:2]
        acc = {0: bank[2][:, 0:512], 1: bank[2][:, 512:1024]}
        misc = [bank[3][:, 0:512], bank[3][:, 512:1024]]

        idx = sb("idx", [P, F], mybir.dt.int32)
        gathered = sb("gathered", [P, F, D])
        e_dmajor = sb("e_dmajor", [P, D, 3, F])
        e_rest = sb("e_rest", [P, D, F])
        e_parts = sb("e_parts", [P, D, P], BF16)
        e_copies = sb("e_copies", [P, 2 * GCOLS])
        e_stack = sb("e_stack", [P, 2 * GCOLS], BF16)
        hidden = sb("hidden", [P, 2, COLS])
        relu0 = sb("relu0", [H, 2, COLS])
        relu1 = sb("relu1", [P, 2, COLS])
        e_shifted = sb("e_shifted", [P, T0, COLS])
        z = sb("z", [P, RING, 2, COLS])
        z_high = sb("z_high", [P, RING, 2, COLS], F32R)
        z_low = sb("z_low", [P, RING, 2, COLS], F32R)

        WIDE = F + SHIFTS - 1
        z_flat = z[:].rearrange("p r t c -> p (r t c)")
        at = [0]
        for size in (F * F, F * WIDE, SHIFTS * F, H * F):
            at.append(at[-1] + size)
        w0_in = z_flat[:, at[0]:at[1]].rearrange("p (h m) -> p h m", h=F)
        w0_sym = z_flat[:, at[1]:at[2]]
        w0_rows = z_flat[:, at[2]:at[3]]
        w1_rows = z_flat[:, at[3]:at[4]]
        w1_in = e_copies[:, 0:H * F].rearrange("p (h m) -> p h m", h=H)
        w_full = sb("w_full", [P, T0 + T1, L])
        w_high = sb("w_high", [P, T0 + T1, L], F32R)
        w_low = sb("w_low", [P, T0 + T1, L], F32R)
        ident = sb("ident", [P, P])
        ident_bf = sb("ident_bf", [P, P], BF16)
        pick = sb("pick", [P, F + 1], BF16)
        pick1 = sb("pick1", [P, T1, 2, H], BF16)
        bias0, bias1 = sb("bias0", [P, 1]), sb("bias1", [P, 1])

        top_a = sb("top_a", [H + C, B])
        top_b = sb("top_b", [P, B])
        dense = relu1[:].rearrange("p x c -> p (x c)")[:, 0:GROUPS * (H + C)] \
            .rearrange("p (g c) -> p g c", g=GROUPS)
        shifted_flat = e_shifted[:].rearrange("p t c -> p (t c)")
        wt1_a, wt1_b = shifted_flat[0:H + C, 0:M1], shifted_flat[:, M1:2 * M1]
        wt2 = shifted_flat[:, 2 * M1:2 * M1 + M1 // P * M2].rearrange("p (t n) -> p t n", n=M2)
        wt3 = sb("wt3", [P, M2 // P])
        bias_t1, bias_t2 = sb("bias_t1", [P, M1 // P]), sb("bias_t2", [P, M2 // P])
        N = B // 2

        def mlp_h1(half_, t):
            c = (half_ * (M1 // P) + t) * N
            return z_flat[:, c:c + N]

        def mlp_h2(half_, t):
            c = (2 * (M1 // P) + half_ * (M2 // P) + t) * N
            return z_flat[:, c:c + N]

        y_row = z_flat[0:1, 2 * (M1 + M2) // P * N:2 * (M1 + M2) // P * N + B]

        s_idx, s_w0, s_w1, s_small, s_top = map(sem, ("s_idx", "s_w0", "s_w1", "s_small", "s_top"))
        s_wtop = sem("s_wtop")
        s_gather = sem("s_gather")
        s_gather_go = sem("s_gather_go")
        s_const = sem("s_const")
        s_zeroed = sem("s_zeroed")
        s_sym = sem("s_sym")
        s_pick = sem("s_pick")
        s_w1_rows = sem("s_w1_rows")
        s_wt = sem("s_wt")
        s_wt_high, s_wt_low = sem("s_wt_high"), sem("s_wt_low")
        s_dense_t, s_dense = sem("s_dense_t"), sem("s_dense")
        s_eprep_act, s_eprep_dve = sem("s_eprep_act"), sem("s_eprep_dve")
        s_etr = sem("s_etr")
        s_eout = sem("s_eout")
        s_spread = sem("s_spread")
        s_shift = [sem(f"s_shift{n}") for n in range((T0 + 1) // 2)]
        s_z = sem("s_z")
        s_high = sem("s_high")
        s_low_dve, s_low_pool = sem("s_low_dve"), sem("s_low_pool")
        s_main = sem("s_main")
        s_read0, s_read1 = sem("s_read0"), sem("s_read1")
        s_hid = sem("s_hid")
        s_sum0, s_sum1 = sem("s_sum0"), sem("s_sum1")
        s_mlp, s_mlp_act, s_out = sem("s_mlp"), sem("s_mlp_act"), sem("s_out")

        E_BANKS = 6
        E_STEP = 21
        E_FILL = {21: (0, 1), 22: (2, 3), 23: (4, 5)}
        E_OUT = {24: (0, 1), 25: (2, 3), 26: (4, 5)}

        WBANKS = [(0, 4, [(K0, 0, 4)]), (4, 3, [(K0, 0, 2), (K0_LAST, 2, 1)])]
        WBANKS += [(T0 + 4 * n, 4, [(P, 0, 4)]) for n in range(T1 // 4 - 1)]
        WBANKS += [(T0 + T1 - 4, 4, [(P, 0, 3), (H, 3, 1)])]

        def wbank(n):
            return spread[n % 4 // 2][:, n % 2 * 512:n % 2 * 512 + 512].rearrange("p (t o) -> p t o", o=L)

        def mlp_bank(n):
            return bank[n // 2][:, n % 2 * 512:n % 2 * 512 + 512]

        IDS_STEP = 30
        PAIRS0, PAIRS1 = len(prologue) // 2, T1 // 2
        L0_AFTER = PAIRS0 + PAIRS1

        def shifts_of(g):
            return sum(min(3, SHIFTS - 3 * t) for t in g.tiles)

        def spread_before(groups, k):
            return sum(g.layer == 1 for g in groups[:k])

        def spread_count(i, groups, k):
            return QB * PAIRS1 * i + spread_before(groups, k)

        def slot_user_before(groups, k):
            users = [n for n in range(k) if groups[n].layer == 1]
            return users[-2] if len(users) > 1 else len(users) - 2 - PAIRS0

        HIGH_PRO, HIGH_BODY = (sum(g.how != NATIVE for g in x) for x in (prologue, loop_body))

        def high_count(i, groups, k):
            start = 0 if groups is prologue else HIGH_PRO + HIGH_BODY * i
            return start + sum(g.how != NATIVE for g in groups[:k + 1])

        def low_count(i, groups, k):
            how = groups[k].how
            start = 0 if groups is prologue else \
                count_before(prologue, PRO, how) + count_before(loop_body, BODY, how) * i
            return start + count_before(groups, k + 1, how)

        def group_count(i, groups, k):
            return k if groups is prologue else PRO + BODY * i + k

        def ring_of(groups, k):
            return (k if groups is prologue else PRO + k) % RING

        def rows_of(g):
            return P if g.layer == 1 else K0_LAST if g.last else K0

        def weight_tile(g, t):
            return t if g.layer == 0 else T0 + t

        def half(i, g):
            return ((i + g.block // QB) % 2) * GCOLS + (g.block % QB) * COLS

        ids_v = ids.rearrange("(g p) f -> g p f", p=P)
        block = ctx.enter_context(nc.Block())

        @block.sync
        def _(sp):
            sp.dma_start(idx[:], ids_v[0]).then_inc(s_idx, 16)
            w0_v = W0.rearrange("o (h m) -> o h m", h=F)
            sp.dma_start(w0_in[0:H], w0_v[H:L]).then_inc(s_w0, 16)
            sp.dma_start(w0_in[H:L], w0_v[0:H]).then_inc(s_w0, 16)
            sp.dma_start(w1_in, W1.rearrange("o (h m) -> o h m", h=H)).then_inc(s_w1, 16)
            b0_v = b0.rearrange("(p a) -> p a", a=1)
            sp.dma_start(bias0[0:H], b0_v[H:L]).then_inc(s_small, 16)
            sp.dma_start(bias0[H:L], b0_v[0:H]).then_inc(s_small, 16)
            sp.dma_start(bias1[:], b1.rearrange("(p a) -> p a", a=1)).then_inc(s_small, 16)
            sp.wait_ge(s_zeroed, 2)
            sp.dma_start(dense[:, :, H:H + C], dense_ctx.rearrange("(g p) c -> p g c", p=P)).then_inc(s_top, 16)
            sp.dma_start(wt3[:], W_top3.rearrange("(p t) n -> p (t n)", p=P)).then_inc(s_top, 16)
            sp.dma_start(bias_t1[:], b_top1.rearrange("(p t) -> p t", p=P)).then_inc(s_top, 16)
            sp.dma_start(bias_t2[:], b_top2.rearrange("(p t) -> p t", p=P)).then_inc(s_top, 16)

            def next_ids(i):
                sp.wait_ge(s_gather, (i + 1) * (16 * F))
                nxt = (i + 1) % GROUPS
                row = ids_v[nxt] if isinstance(i, int) else ids_v[bass.ds(nxt, 1)].rearrange("g p f -> p (g f)")
                sp.dma_start(idx[:], row).then_inc(s_idx, 16)

            def shift_e(i, groups, k):
                g = groups[k]
                if not (groups is prologue and g.block == 0):
                    before = group_count(i, groups, k) - (L0_AFTER if groups is not prologue else len(tiles0) // 2 + 1)
                    sp.wait_ge(s_z, before + 1)
                if g.first:
                    sp.wait_ge(s_eout, E_BANKS * (i + g.block // QB) + 4)
                start = half(i, g)
                for t in g.tiles:
                    for j in range(min(3, SHIFTS - 3 * t)):
                        rows = slice(3 * t + j, 3 * t + j + F)
                        src = e_copies[rows, start:start + COLS] if isinstance(start, int) else \
                            e_copies[rows, bass.ds(start, COLS)]
                        sp.dma_start(e_shifted[j * F:(j + 1) * F, t], src).then_inc(s_shift[g.tiles[0] // 2], 16)

            next_ids(0)
            for k in range(PRO):
                shift_e(0, prologue, k)

            def body(i, groups):
                for k, g in enumerate(groups):
                    if g.layer == 0:
                        shift_e(i, groups, k)
                    if groups is loop_body and k == IDS_STEP:
                        next_ids(i + 1)

            with sp.Fori(0, GROUPS - 1) as i:
                body(i, loop_body)
            body(GROUPS - 1, last_body)
            last0 = max(k for k, g in enumerate(last_body) if g.layer == 0)
            sp.wait_ge(s_z, group_count(GROUPS - 1, last_body, last0) + 1)
            sp.dma_start(wt1_a[0:H], W_top1[0:H]).then_inc(s_wtop, 16)
            sp.dma_start(wt1_a[H:H + C], W_top1[H + L:H + L + C]).then_inc(s_wtop, 16)
            sp.dma_start(wt1_b, W_top1[H:H + L]).then_inc(s_wtop, 16)
            sp.dma_start(wt2, W_top2.rearrange("(p t) n -> p t n", p=P)).then_inc(s_wtop, 16)
            sp.wait_ge(s_idx, 16 * (GROUPS + 1))
            sp.wait_ge(s_mlp_act, 14)
            sp.dma_start(out.rearrange("b a -> a b"), y_row[:]).then_inc(s_out, 16)
            sp.wait_ge(s_out, 16)

        @block.gpsimd
        def _(pool):
            for tile in (ident, ident_bf, pick):
                pool.memset(tile[:], 0.0).then_inc(s_const, 1)
            pool.wait_ge(s_const, 3)
            for tile in (ident, ident_bf):
                pool.affine_select(out=tile[:], in_=tile[:], compare_op=ALU.not_equal, fill=1.0, base=0,
                                   pattern=[[-1, P]], channel_multiplier=1).then_inc(s_const, 1)
            for part in range(PARTS):
                pool.wait_ge(s_const, 5 + part)
                pool.affine_select(out=pick[:, 0:F + 1], in_=pick[:, 0:F + 1], compare_op=ALU.not_equal,
                                   fill=1.0, base=-part, pattern=[[-PARTS, F + 1]],
                                   channel_multiplier=1).then_inc(s_const, 1)

            def gather(f):
                pool.indirect_dma_start(gathered[:, f, :], None, tables[f],
                                        bass.IndirectOffsetOnAxis(idx[:, f:f + 1].bitcast(U32), 0)
                                        ).then_inc(s_gather, 16)

            def low_part(i, groups, k):
                g = groups[k]
                r, n, rows = ring_of(groups, k), len(g.tiles), rows_of(g)
                pool.wait_ge(s_high, high_count(i, groups, k))
                pool.tensor_tensor(z_low[0:rows, r, 0:n], z[0:rows, r, 0:n],
                                   z_high[0:rows, r, 0:n].bitcast(F32), ALU.subtract).then_inc(s_low_pool, 1)

            pool.wait_ge(s_idx, 16)
            for f in range(F):
                gather(f)

            def body(i, groups, gathers):
                if gathers:
                    pool.wait_ge(s_idx, 16 * (i + 2))
                    pool.wait_ge(s_eprep_act, 3 * (i + 1))
                    pool.sem_inc(s_gather_go, 1)
                    for f in range(F):
                        gather(f)
                for k, g in enumerate(groups):
                    if g.how == BY_POOL:
                        low_part(i, groups, k)

            with pool.Fori(0, GROUPS - 1) as i:
                body(i, loop_body, True)
            body(GROUPS - 1, last_body, False)

        @block.scalar
        def _(act):
            def e_split(i, step):
                part = lambda n: e_parts[:, :, 0:PARTS * F].rearrange("p d (f n) -> p d f n", n=PARTS)[:, :, :, n]
                if step == 0:
                    act.wait_ge(s_gather, (16 * F) * (i + 1))
                    act.activation(e_dmajor[:], gathered[:].rearrange("p f (d o) -> p d o f", o=1)
                                   .broadcast_to([P, D, 3, F]), ACT.Copy).then_inc(s_eprep_act, 1)
                    act.activation(part(0), gathered[:].rearrange("p f d -> p d f"), ACT.Copy).then_inc(s_eprep_act, 1)
                else:
                    act.wait_ge(s_eprep_dve, 2 * i + 1)
                    act.activation(part(1), e_rest[:], ACT.Copy).then_inc(s_eprep_act, 1)

            def e_out(i, n):
                act.wait_ge(s_etr, E_BANKS * i + n + 1)
                dims, src = (4, misc[n % 2][0:K0]) if n < 4 else (8, misc[n % 2].bitcast(BF16))
                d0 = dims * (n if n < 4 else n - 4)
                rows, to = (K0, e_copies) if n < 4 else (P, e_stack)
                dst = to[0:rows, bass.ds((i % 2) * GCOLS, GCOLS)] if not isinstance(i, int) else \
                    to[0:rows, (i % 2) * GCOLS:(i % 2 + 1) * GCOLS]
                act.activation(dst.rearrange("p (q d b) -> p d q b", q=QB, d=D)[:, d0:d0 + dims],
                               src.rearrange("p (d q b) -> p d q b", d=dims, q=QB), ACT.Copy).then_inc(s_eout, 1)

            def high_part(i, groups, k):
                g = groups[k]
                if g.how == NATIVE:
                    return
                r, n, rows = ring_of(groups, k), len(g.tiles), rows_of(g)
                act.wait_ge(s_z, group_count(i, groups, k) + 1)
                act.activation(z_high[0:rows, r, 0:n], z[0:rows, r, 0:n], ACT.Copy).then_inc(s_high, 1)

            def read_sums0(c_even, done):
                b = c_even
                act.wait_ge(s_main, done)
                act.activation(hidden[H:L, b], acc[0][H:L], ACT.Relu, bias=bias0[H:L]).then_inc(s_read0, 1)
                act.activation(relu0[:, b], acc[0][0:H], ACT.Relu, bias=bias0[0:H]).then_inc(s_read0, 1)

            def copy_hidden(b, done):
                act.wait_ge(s_read0, done)
                act.activation(hidden[0:H, b], hidden[H:L, b], ACT.Copy).then_inc(s_hid, 1)

            def read_sums1(b, done):
                act.wait_ge(s_main, done)
                act.activation(relu1[:, b], acc[1], ACT.Relu, bias=bias1[:]).then_inc(s_read1, 1)

            act.wait_ge(s_w1, 16)
            act.activation(w1_rows.rearrange("p (m h) -> p m h", h=H), w1_in.rearrange("p h m -> p m h"),
                           ACT.Copy).then_inc(s_w1_rows, 1)
            act.wait_ge(s_zeroed, 5)
            for n, (w, cnt, rows) in enumerate(WBANKS):
                act.wait_ge(s_wt, n + 1)
                for rr, c0, cc in rows:
                    ins = act.activation(w_high[0:rr, w + c0:w + c0 + cc], wbank(n)[0:rr, c0:c0 + cc], ACT.Copy)
                ins.then_inc(s_wt_high, 1)
            act.wait_ge(s_small, 48)
            act.nop().then_inc(s_read1, 1)
            e_split(0, 0)
            e_split(0, 1)
            for n in range(E_BANKS):
                e_out(0, n)
            act.wait_ge(s_dense_t, 1)
            dv = top_a[H:H + C].rearrange("c (x b) -> c x b", x=2)
            act.activation(dv[:, 0], misc[0][H:H + C], ACT.Copy).then_inc(s_dense, 1)
            act.activation(dv[:, 1], misc[1][H:H + C], ACT.Copy).then_inc(s_dense, 1)

            after = LEAD - 1
            for k, g in enumerate(prologue):
                high_part(0, prologue, k)
                if k - after >= 0 and prologue[k - after].last:
                    read_sums0(0, k - after + 1)
                    copy_hidden(0, 1)

            def body(i, groups):
                for k, g in enumerate(groups):
                    high_part(i, groups, k)
                    if k == after - 1:
                        read_sums0(1, group_count(i, groups, 0))
                        copy_hidden(1, 2 * (i * QB + 2) - 1)
                    j = k - after
                    if j >= 0 and groups[j].last:
                        done = group_count(i, groups, j) + 1
                        if groups[j].layer == 1:
                            read_sums1(groups[j].block % 2, done)
                        else:
                            c = groups[j].block
                            read_sums0(c % 2, done)
                            copy_hidden(c % 2, 2 * (i * QB + c + 1) - 1)
                    if groups is loop_body:
                        if k == E_STEP:
                            e_split(i + 1, 0)
                        if k == E_STEP + 2:
                            e_split(i + 1, 1)
                        if k in E_OUT:
                            for n in E_OUT[k]:
                                e_out(i + 1, n)

            with act.Fori(0, GROUPS - 1) as i:
                body(i, loop_body)
            body(GROUPS - 1, last_body)
            read_sums1(1, group_count(GROUPS - 1, last_body, len(last_body)))

            for n in range(M1 // P * 2):
                hf, t = divmod(n, M1 // P)
                act.wait_ge(s_mlp, n + 1)
                act.activation(mlp_h1(hf, t), mlp_bank(n), ACT.Relu, bias=bias_t1[:, t:t + 1]).then_inc(s_mlp_act, 1)
            for n in range(M2 // P * 2):
                hf, t = divmod(n, M2 // P)
                act.wait_ge(s_mlp, 8 + n + 1)
                act.activation(mlp_h2(hf, t), mlp_bank(n), ACT.Relu, bias=bias_t2[:, t:t + 1]).then_inc(s_mlp_act, 1)
            for hf in range(2):
                act.wait_ge(s_mlp, 12 + hf + 1)
                act.activation(y_row[0:1, hf * 512:(hf + 1) * 512], mlp_bank(4 + hf)[0:1], ACT.Copy).then_inc(s_mlp_act, 1)

        @block.vector
        def _(dve):
            dve.memset(e_parts[:], 0.0).then_inc(s_zeroed, 1)
            dve.memset(dense, 0.0).then_inc(s_zeroed, 1)
            for w in (w_full, w_high, w_low):
                dve.memset(w[:, T0 + T1 - 1].bitcast(F32), 0.0).then_inc(s_zeroed, 1)
            dve.wait_ge(s_w0, 32)
            sym = w0_sym.rearrange("p (h m) -> p h m", m=WIDE)
            dve.tensor_tensor(sym[:, :, 0:F], w0_in, w0_in.rearrange("p h m -> p m h"), ALU.add).then_inc(s_sym, 1)
            diagonal = w0_sym[:, 0:(WIDE + 1) * (F - 1) + 1:WIDE + 1]
            dve.wait_ge(s_sym, 1)
            dve.tensor_scalar(diagonal, diagonal, 0.5, None, ALU.mult).then_inc(s_sym, 1)
            dve.wait_ge(s_sym, 2)
            dve.tensor_copy(sym[:, :, F:WIDE], sym[:, :, 0:WIDE - F]).then_inc(s_sym, 1)
            dve.wait_ge(s_sym, 3)
            windows = bass.AP(w0_sym.tensor, w0_sym.offset, [w0_sym.ap[0], [1, SHIFTS], [WIDE + 1, F]])
            dve.tensor_copy(w0_rows.rearrange("p (s h) -> p s h", h=F), windows).then_inc(s_sym, 1)
            dve.wait_ge(s_const, 5 + PARTS)
            dve.tensor_copy(pick1[:], pick[:, 0:F + 1].rearrange("p (t j o) -> p t j o", j=2, o=1)
                            .broadcast_to([P, T1, 2, H])).then_inc(s_pick, 1)
            dve.wait_ge(s_zeroed, 5)
            for n, (w, cnt, rows) in enumerate(WBANKS):
                dve.wait_ge(s_wt_high, n + 1)
                for rr, c0, cc in rows:
                    dve.tensor_copy(w_full[0:rr, w + c0:w + c0 + cc], wbank(n)[0:rr, c0:c0 + cc])
                    ins = dve.tensor_tensor(w_low[0:rr, w + c0:w + c0 + cc], wbank(n)[0:rr, c0:c0 + cc],
                                            w_high[0:rr, w + c0:w + c0 + cc].bitcast(F32), ALU.subtract)
                ins.then_inc(s_wt_low, 1)

            def e_rest_of(i, step):
                part = lambda n: e_parts[:, :, 0:PARTS * F].rearrange("p d (f n) -> p d f n", n=PARTS)[:, :, :, n]
                if step == 0:
                    dve.wait_ge(s_eprep_act, 3 * i + 2)
                    dve.tensor_tensor(e_rest[:], e_dmajor[:, :, 0], part(0), ALU.subtract).then_inc(s_eprep_dve, 1)
                else:
                    dve.wait_ge(s_eprep_act, 3 * i + 3)
                    dve.tensor_tensor(part(2), e_rest[:], part(1), ALU.subtract).then_inc(s_eprep_dve, 1)

            def form_z(i, groups, k):
                g = groups[k]
                r, n, rows = ring_of(groups, k), len(g.tiles), rows_of(g)
                if not (groups is prologue and k < RING):
                    dve.wait_ge(s_main, group_count(i, groups, k) - RING + 1)
                if g.layer == 1 and g.first:
                    dve.wait_ge(s_hid, i * QB + g.block + 1)
                if g.layer == 1:
                    kept = hidden[:, g.block % 2]
                    slot = spread_before(groups, k) % 2
                    dve.wait_ge(s_spread, spread_count(i, groups, k) + 1)
                    other = spread[slot][:, 0:n * COLS].rearrange("p (t c) -> p t c", t=n)
                else:
                    start = half(i, g)
                    kept = e_copies[0:rows, start:start + COLS] if isinstance(start, int) else \
                        e_copies[0:rows, bass.ds(start, COLS)]
                    dve.wait_ge(s_shift[g.tiles[0] // 2], 16 * shifts_of(g) * (i * QB + g.block + 1))
                    other = e_shifted[0:rows, g.tiles[0]:g.tiles[-1] + 1]
                kept = kept.rearrange("p (o c) -> p o c", o=1).broadcast_to([rows, n, COLS])
                dve.tensor_tensor(z[0:rows, r, 0:n], other, kept, ALU.mult).then_inc(s_z, 1)

            def low_part(i, groups, k):
                g = groups[k]
                if g.how != BY_DVE:
                    return
                r, n, rows = ring_of(groups, k), len(g.tiles), rows_of(g)
                dve.wait_ge(s_high, high_count(i, groups, k))
                dve.tensor_tensor(z_low[0:rows, r, 0:n], z[0:rows, r, 0:n],
                                  z_high[0:rows, r, 0:n].bitcast(F32), ALU.subtract).then_inc(s_low_dve, 1)

            def sum_dims(layer, b, done, column):
                src, rows, to = (relu0, H, top_a) if layer == 0 else (relu1, P, top_b)
                dve.wait_ge(s_read0 if layer == 0 else s_read1, done)
                dst = to[0:rows, column:column + RB] if isinstance(column, int) else to[0:rows, bass.ds(column, RB)]
                dve.tensor_reduce(dst, src[:, b].rearrange("p (d b) -> p b d", d=D), AX_X, ALU.add) \
                   .then_inc(s_sum0 if layer == 0 else s_sum1, 1)

            e_rest_of(0, 0)
            e_rest_of(0, 1)
            for k in range(PRO):
                form_z(0, prologue, k)
                if k:
                    low_part(0, prologue, k - 1)
            after = LEAD

            def body(i, groups):
                for k, g in enumerate(groups):
                    form_z(i, groups, k)
                    if k:
                        low_part(i, groups, k - 1)
                    if k == after:
                        sum_dims(0, 1, 2 * (i * QB + 2), i * P + RB)
                    if k == after + 1:
                        sum_dims(0, 0, 2 * (i * QB + 1), i * P)
                    j = k - after
                    if j >= 0 and groups[j].last:
                        c = groups[j].block
                        if groups[j].layer == 1:
                            sum_dims(1, c % 2, i * QB + c + 2, i * P + c * RB)
                        elif c < QB:
                            sum_dims(0, c % 2, 2 * (i * QB + c + 1), i * P + c * RB)
                    if groups is loop_body:
                        if k == E_STEP + 1:
                            e_rest_of(i + 1, 0)
                        if k == E_STEP + 3:
                            e_rest_of(i + 1, 1)
                low_part(i, groups, len(groups) - 1)

            with dve.Fori(0, GROUPS - 1) as i:
                body(i, loop_body)
            body(GROUPS - 1, last_body)
            c = GROUPS * QB - 1
            sum_dims(1, 1, c + 2, c * RB)

        @block.tensor
        def _(pe):
            pe.wait_ge(s_const, 5)
            pe.wait_ge(s_sym, 4)
            for n, (w, cnt, rows) in enumerate(WBANKS):
                if n == 2:
                    pe.wait_ge(s_w1_rows, 1)
                if n >= 4:
                    pe.wait_ge(s_wt_low, n - 3)
                for t in range(cnt):
                    if w < T0:
                        c, size = (w + t) * K0, K0 if w + t < T0 - 1 else K0_LAST
                        src = w0_rows[:, c:c + size]
                    else:
                        c = (w - T0 + t) * P
                        size = min(P, H * F - c)
                        src = w1_rows[:, c:c + size]
                    ins = pe.transpose(wbank(n)[0:size, t], src, ident[:])
                ins.then_inc(s_wt, 1)

            def e_transpose(i, n):
                if not (isinstance(i, int) and i == 0 and n < 2):
                    pe.wait_ge(s_eout, E_BANKS * i + n - 1)
                if n < 4:
                    pe.wait_ge(s_eprep_act, 3 * i + 1)
                    for d in range(4):
                        src = e_dmajor[:, 4 * n + d].rearrange("p o f -> p (o f)")
                        ins = pe.transpose(misc[n % 2][0:K0, d * P:(d + 1) * P], src, ident[:])
                else:
                    pe.wait_ge(s_eprep_dve, 2 * i + 2)
                    bank16 = misc[n % 2].bitcast(BF16)
                    for d in range(8):
                        ins = pe.transpose(bank16[:, d * P:(d + 1) * P], e_parts[:, 8 * (n - 4) + d], ident_bf[:])
                ins.then_inc(s_etr, 1)

            def spread_group(i, groups, k):
                g = groups[k]
                if g.layer == 0:
                    return
                slot = spread_before(groups, k) % 2
                before = group_count(i, groups, slot_user_before(groups, k))
                pe.wait_ge(s_z, before + 1)
                if g.first and g.block == 0:
                    pe.wait_ge(s_eout, E_BANKS * (i + 1))
                start = half(i, g)
                moving = e_stack[:, start:start + COLS] if isinstance(start, int) else e_stack[:, bass.ds(start, COLS)]
                for x, t in enumerate(g.tiles):
                    ins = pe.matmul(spread[slot][:, x * COLS:(x + 1) * COLS],
                                    pick1[:, t].rearrange("p j h -> p (j h)"), moving, start=True, stop=True)
                ins.then_inc(s_spread, 1)

            def multiply(i, groups, k):
                g = groups[k]
                r = ring_of(groups, k)
                if g.first and not (groups is prologue and k == 0):
                    c = i * QB + g.block
                    if g.layer == 0:
                        pe.wait_ge(s_read0, 2 * c)
                    else:
                        pe.wait_ge(s_read1, c + 1)
                passes = [(w_full, z, s_z, group_count(i, groups, k) + 1)]
                if g.how != NATIVE:
                    low = s_low_dve if g.how == BY_DVE else s_low_pool
                    passes = [(w_high, z_high, s_high, high_count(i, groups, k)),
                              (w_low, z_high, None, None),
                              (w_high, z_low, low, low_count(i, groups, k))]
                for n, (w, moving, ready, value) in enumerate(passes):
                    if ready is not None:
                        pe.wait_ge(ready, value)
                    for x, t in enumerate(g.tiles):
                        kk = rows_of(g)
                        ins = pe.matmul(acc[g.layer], w[0:kk, weight_tile(g, t)], moving[0:kk, r, x],
                                        start=g.first and n == 0 and x == 0,
                                        stop=g.last and n == len(passes) - 1 and x == len(g.tiles) - 1)
                ins.then_inc(s_main, 1)

            for n in range(E_BANKS):
                e_transpose(0, n)
            pe.wait_ge(s_top, 64)
            pe.wait_ge(s_eout, E_BANKS)
            for gi in range(GROUPS):
                ins = pe.transpose(misc[gi // 4][0:H + C, (gi % 4) * P:(gi % 4 + 1) * P], dense[:, gi], ident[:])
            ins.then_inc(s_dense_t, 1)
            pe.wait_ge(s_wt_low, len(WBANKS))
            pe.wait_ge(s_pick, 1)

            for k in range(PRO):
                if k + LEAD >= PRO:
                    spread_group(0, loop_body, k + LEAD - PRO)
                multiply(0, prologue, k)

            def body(i, groups):
                for k in range(len(groups)):
                    if k + LEAD < len(groups):
                        spread_group(i, groups, k + LEAD)
                    elif groups is loop_body:
                        spread_group(i + 1, loop_body, k + LEAD - BODY)
                    multiply(i, groups, k)
                    if groups is loop_body and k in E_FILL:
                        for n in E_FILL[k]:
                            e_transpose(i + 1, n)

            with pe.Fori(0, GROUPS - 1) as i:
                body(i, loop_body)
            body(GROUPS - 1, last_body)

            for hf in range(2):
                if hf == 0:
                    pe.wait_ge(s_dense, 2)
                    pe.wait_ge(s_wtop, 64)
                    pe.wait_ge(s_read1, GROUPS * QB + 1)
                pe.wait_ge(s_sum1, (hf + 1) * GROUPS * QB // 2)
                pe.wait_ge(s_sum0, (hf + 1) * GROUPS * QB // 2)
                for t in range(M1 // P):
                    o = mlp_bank(hf * (M1 // P) + t)
                    pe.matmul(o, wt1_a[:, t::M1 // P], top_a[:, hf * N:(hf + 1) * N], start=True, stop=False)
                    pe.matmul(o, wt1_b[:, t::M1 // P], top_b[:, hf * N:(hf + 1) * N],
                              start=False, stop=True).then_inc(s_mlp, 1)
            for hf in range(2):
                for t in range(M2 // P):
                    for kt in range(M1 // P):
                        if t == 0:
                            pe.wait_ge(s_mlp_act, hf * (M1 // P) + kt + 1)
                        ins = pe.matmul(mlp_bank(hf * (M2 // P) + t), wt2[:, kt, t::M2 // P], mlp_h1(hf, kt),
                                        start=kt == 0, stop=kt == M1 // P - 1)
                    ins.then_inc(s_mlp, 1)
            for hf in range(2):
                for kt in range(M2 // P):
                    pe.wait_ge(s_mlp_act, 8 + hf * (M2 // P) + kt + 1)
                    ins = pe.matmul(mlp_bank(4 + hf)[0:1], wt3[:, kt:kt + 1], mlp_h2(hf, kt),
                                    start=kt == 0, stop=kt == M2 // P - 1)
                ins.then_inc(s_mlp, 1)


def kernel(**inputs):
    import numpy as np
    import concourse.bacc as bacc
    from concourse.bass_utils import run_bass_kernel_spmd

    nc = bacc.Bacc("TRN2", target_bir_lowering=False, num_devices=1)
    arrays, aps = {}, {}
    for name, value in inputs.items():
        a = np.ascontiguousarray(value)
        arrays[f"in_{name}"] = a
        aps[name] = nc.dram_tensor(f"in_{name}", a.shape, mybir.dt.from_np(a.dtype), kind="ExternalInput").ap()
    rows, fields = inputs["ids"].shape
    out = nc.dram_tensor("out_y", (rows, 1), F32, kind="ExternalOutput").ap()
    dlrm_kernel(nc, aps["dense_ctx"], aps["ids"], [aps[f"tbl_{f}"] for f in range(fields)],
                aps["W_top1"], aps["b_top1"], aps["W_top2"], aps["b_top2"], aps["W_top3"],
                aps["L0_rec_W0"], aps["L0_rec_b0"], aps["L0_rec_W1"], aps["L0_rec_b1"], out)
    r = run_bass_kernel_spmd(nc, [arrays], core_ids=[0])
    return r.results[0]["out_y"]
```

```python
from contextlib import ExitStack

import concourse.bass as bass
from concourse import mybir

F32 = mybir.dt.float32
F32R = mybir.dt.float32r
BF16 = mybir.dt.bfloat16
U32 = mybir.dt.uint32
ACT = mybir.ActivationFunctionType
ALU = mybir.AluOpType
AX_X = mybir.AxisListType.X

P = 128
RING = 7
RING_LOW = 4
BY_DMA = (2, 4, 7, 9)
LEAD = 4
ACT_AFTER = 3
DVE_AFTER = 4
E_STEP = 24
E_REST = 1
E_GAP = 0
E_NEXT = 1
E_GAP2 = 3
IDS_STEP = 20
G_MARGIN = 5
P_WEIGHT = 0.1
NATIVE, BY_DVE, BY_POOL = "native", "low part by VectorE", "low part by GpSimd"


PROLOGUE_HOW = "NDDN NNDN"
LOOP_HOW = ("DPNNPNDDPN DPND"
            "DPNPNNPDPD PPDP"
            "NDNDPPDNNP NDPP"
            "DNNDPNNPPD DPNN")
LAST_HOW = ("DPNPDPNPDP PDPP"
            "NDNPNPDPNP PDPP"
            "PDPPDDNNPP"
            "DPDPPPDPDP")


class Group:

    def __init__(self, layer, block, tiles, first, last):
        self.layer, self.block, self.tiles, self.first, self.last = layer, block, tiles, first, last
        self.how = NATIVE
        place = tiles[0] // 2
        self.refilled = place in BY_DMA if layer else block > 1
        self.buffer = place if layer == 0 else BY_DMA.index(place) if place in BY_DMA else None


def layer_groups(layer, block, tiles):
    pairs = [tiles[t:t + 2] for t in range(0, len(tiles), 2)]
    return [Group(layer, block, p, p is pairs[0], p is pairs[-1]) for p in pairs]


def gather_steps(groups, fields, e_step):
    steps = list(range(e_step + 1, len(groups))) + list(range(e_step - G_MARGIN))
    weights = [P_WEIGHT if groups[k].how == BY_POOL else 1.0 for k in steps]
    found, early, f, run = {}, 0, 0, 0.0
    for k, weight in zip(steps, weights):
        run += weight
        upto = round(fields * run / sum(weights))
        found[k] = range(f, upto)
        f = upto
        if k > e_step:
            early = f
    return found, early


def dlrm_kernel(nc, dense_ctx, ids, tables, W_top1, b_top1, W_top2, b_top2, W_top3, W0, b0, W1, b1, out):
    B, F = ids.shape
    D = tables[0].shape[1]
    L = W0.shape[0]
    H = L // 2
    C = dense_ctx.shape[1]
    M1, M2 = W_top1.shape[1], W_top2.shape[1]
    GROUPS = B // P
    QB = 4
    RB = P // QB
    COLS = RB * D
    GCOLS = QB * COLS
    SHIFTS = F // 2 + 1
    T0 = -(-SHIFTS // 3)
    T1 = -(-F // 2)
    K0 = 3 * F
    K0_LAST = (SHIFTS - 3 * (T0 - 1)) * F
    PARTS = 3
    assert L == P and COLS == 512 and PARTS * F <= P and K0 <= P

    tiles0, tiles1 = list(range(T0)), list(range(T1))
    prologue = layer_groups(0, 0, tiles0) + layer_groups(0, 1, tiles0)

    def body_groups(ends):
        found = []
        for q in range(QB):
            found += layer_groups(1, q, tiles1)
            if not (ends and q + 2 >= QB):
                found += layer_groups(0, q + 2, tiles0)
        return found

    loop_body, last_body = body_groups(False), body_groups(True)
    PRO, BODY = len(prologue), len(loop_body)
    assert BODY % RING == 0 and BODY % RING_LOW == 0

    HOW = {"N": NATIVE, "D": BY_DVE, "P": BY_POOL}
    for groups, letters in ((prologue, PROLOGUE_HOW), (loop_body, LOOP_HOW), (last_body, LAST_HOW)):
        letters = letters.replace(" ", "")
        assert len(letters) == len(groups)
        for g, letter in zip(groups, letters):
            g.how = HOW[letter]

    def count_before(groups, k, how):
        return sum(g.how == how for g in groups[:k])

    with ExitStack() as ctx:
        def sb(name, shape, dt=F32):
            return ctx.enter_context(nc.sbuf_tensor(name, shape, dt))

        def sem(name):
            return ctx.enter_context(nc.semaphore(name))

        bank = [ctx.enter_context(nc.psum_tensor(f"bank{n}", [P, 1024], F32)) for n in range(4)]
        spread = bank[0:2]
        acc = {0: bank[2][:, 0:512], 1: bank[2][:, 512:1024]}
        misc = [bank[3][:, 0:512], bank[3][:, 512:1024]]

        idx = sb("idx", [P, F], mybir.dt.int32)
        gathered = sb("gathered", [P, F, D])
        e_parts = sb("e_parts", [P, D, P], BF16)
        e_copies = sb("e_copies", [P, 2 * GCOLS])
        e_stack = sb("e_stack", [P, 2 * GCOLS], BF16)
        hidden = sb("hidden", [P, 2, COLS])
        relu0 = sb("relu0", [H, COLS])
        relu1 = sb("relu1", [P, COLS])
        e1_shifted = sb("e1_shifted", [P, len(BY_DMA), 2, COLS])
        e_shifted = sb("e_shifted", [P, T0, 2 * COLS])
        z = sb("z", [P, RING, 2, COLS])
        z_high = sb("z_high", [P, RING, 2, COLS], F32R)
        z_low = sb("z_low", [P, RING_LOW, 2, COLS], F32R)

        WIDE = F + SHIFTS - 1
        z_flat = z[:].rearrange("p r t c -> p (r t c)")
        at = [0]
        for size in (F * F, F * WIDE, SHIFTS * F, H * F):
            at.append(at[-1] + size)
        w0_in = z_flat[:, at[0]:at[1]].rearrange("p (h m) -> p h m", h=F)
        w0_sym = z_flat[:, at[1]:at[2]]
        w0_rows = z_flat[:, at[2]:at[3]]
        w1_rows = z_flat[:, at[3]:at[4]]
        w1_in = e_copies[:, 0:H * F].rearrange("p (h m) -> p h m", h=H)
        WIDE1 = 2 * F - 1
        w1_wide = [(0, F, e_shifted[:].rearrange("p t c -> p (t c)")[:, 0:F * WIDE1]),
                   (F, H, e1_shifted[:].rearrange("p n t c -> p (n t c)")[:, 0:(H - F) * WIDE1])]
        w_full = sb("w_full", [P, T0 + T1, L])
        w_high = sb("w_high", [P, T0 + T1, L], F32R)
        w_low = sb("w_low", [P, T0 + T1, L], F32R)
        ident = relu1[:, 0:P]
        ident_bf = sb("ident_bf", [P, P], BF16)
        pick = sb("pick", [P, F], BF16)
        pick_wide = sb("pick_wide", [P, 3, F], BF16)
        runs1 = []
        for t in tiles1:
            if t // 2 not in BY_DMA:
                if runs1 and runs1[-1][-1] == t - 1:
                    runs1[-1].append(t)
                else:
                    runs1.append([t])
        picked1 = [t for run in runs1 for t in run]
        pick1 = sb("pick1", [P, len(picked1), 2, H], BF16)
        bias0, bias1 = sb("bias0", [P, 1]), sb("bias1", [P, 1])

        top_a = sb("top_a", [H + C, B])
        top_b = sb("top_b", [P, B])
        dense = hidden[:].rearrange("p x c -> p (x c)")[:, 0:GROUPS * (H + C)] \
            .rearrange("p (g c) -> p g c", g=GROUPS)
        pick0 = top_b[:].bitcast(BF16)[:, 0:3 * T0 * F] \
            .rearrange("p (s f) -> p s f", f=F)
        shifted_flat = e_shifted[:].rearrange("p t c -> p (t c)")
        wt1_a, wt1_b = shifted_flat[0:H + C, 0:M1], shifted_flat[:, M1:2 * M1]
        wt2 = shifted_flat[:, 2 * M1:2 * M1 + M1 // P * M2].rearrange("p (t n) -> p t n", n=M2)
        wt3 = sb("wt3", [P, M2 // P])
        ones = sb("ones", [P, 1])
        bias_t1, bias_t2 = sb("bias_t1", [P, M1 // P]), sb("bias_t2", [P, M2 // P])
        N = B // 2

        def mlp_h1(half_, t):
            c = (half_ * (M1 // P) + t) * N
            return z_flat[:, c:c + N]

        high_flat = z_high[:].rearrange("p r t c -> p (r t c)")
        low_flat = z_low[:].rearrange("p r t c -> p (r t c)")

        def mlp_h1_part(half_, t, low):
            c = (half_ * (M1 // P) + t) * N
            return (low_flat if low else high_flat)[:, c:c + N]

        def wt2_part(low):
            c = 2 * M1 // P * N + (M1 // P * M2 if low else 0)
            return high_flat[:, c:c + M1 // P * M2].rearrange("p (t n) -> p t n", n=M2)

        def mlp_h2(half_, t):
            c = (2 * (M1 // P) + half_ * (M2 // P) + t) * N
            return z_flat[:, c:c + N]

        def mlp_weighted(half_, t):
            return w_full[:].rearrange("p t o -> p (t o)")[:, (half_ * (M2 // P) + t) * N:][:, 0:N]

        y_row = z_flat[0:1, 2 * (M1 + M2) // P * N:2 * (M1 + M2) // P * N + B]

        s_idx, s_w0, s_w1, s_small, s_top = map(sem, ("s_idx", "s_w0", "s_w1", "s_small", "s_top"))
        s_wtop = sem("s_wtop")
        s_gather = sem("s_gather")
        s_gather_go = sem("s_gather_go")
        s_refill_go = sem("s_refill_go")
        s_const = sem("s_const")
        s_zeroed = sem("s_zeroed")
        s_sym = sem("s_sym")
        s_pick = sem("s_pick")
        s_w1_rows = sem("s_w1_rows")
        s_wt = sem("s_wt")
        s_wt_high, s_wt_low = sem("s_wt_high"), sem("s_wt_low")
        s_dense_t, s_dense = sem("s_dense_t"), sem("s_dense")
        s_eprep_act, s_eprep_dve = sem("s_eprep_act"), sem("s_eprep_dve")
        s_etr = sem("s_etr")
        s_eout = sem("s_eout")
        s_spread = sem("s_spread")
        s_shift = [sem(f"s_shift{n}") for n in range((T0 + 1) // 2)]
        s_shift1 = [sem(f"s_shift1_{n}") for n in range(len(BY_DMA))]
        s_z = sem("s_z")
        s_high = sem("s_high")
        s_low_dve, s_low_pool = sem("s_low_dve"), sem("s_low_pool")
        s_main = sem("s_main")
        s_read0, s_read1 = sem("s_read0"), sem("s_read1")
        s_hid = sem("s_hid")
        s_sum0, s_sum1 = sem("s_sum0"), sem("s_sum1")
        s_mlp, s_mlp_act, s_out = sem("s_mlp"), sem("s_mlp_act"), sem("s_out")
        s_weighted = sem("s_weighted")
        s_wt2_high, s_wt2_low = sem("s_wt2_high"), sem("s_wt2_low")
        s_h1_high, s_h1_low = sem("s_h1_high"), sem("s_h1_low")
        s_h1_low_pool = sem("s_h1_low_pool")

        E_BANKS = 6
        E_FILL = {E_STEP + E_GAP + E_NEXT * n: (2 * n, 2 * n + 1) for n in range(3)}
        E_OUT = {k + E_GAP2: banks for k, banks in E_FILL.items()}

        GATHERS, EARLY = gather_steps(loop_body, F, E_STEP)

        WBANKS = [(0, 4, [(K0, 0, 4)]), (4, 3, [(K0, 0, 2), (K0_LAST, 2, 1)])]
        WBANKS += [(T0 + 4 * n, 4, [(P, 0, 4)]) for n in range(T1 // 4 - 1)]
        WBANKS += [(T0 + T1 - 4, 4, [(P, 0, 3), (H, 3, 1)])]

        def wbank(n):
            return spread[n % 4 // 2][:, n % 2 * 512:n % 2 * 512 + 512].rearrange("p (t o) -> p t o", o=L)

        def e_bank(i, n):
            return spread[1][:, n * 512:n * 512 + 512] if isinstance(i, int) and n < 2 else misc[n % 2]

        def mlp_bank(n):
            return bank[n // 2][:, n % 2 * 512:n % 2 * 512 + 512]

        PAIRS0, PAIRS1 = len(prologue) // 2, T1 // 2

        def shifts_of(g):
            if g.layer == 0:
                return [(t, j, F) for t in g.tiles for j in range(min(3, SHIFTS - 3 * t))]
            return [(t, j, H) for t in g.tiles for j in range(2)]

        def shift_sem(g):
            return (s_shift if g.layer == 0 else s_shift1)[g.buffer]

        def spread_before(groups, k):
            return sum(not g.refilled for g in groups[:k])

        def spread_count(i, groups, k):
            return k if groups is prologue else PRO + spread_before(loop_body, BODY) * i + spread_before(groups, k)

        def slot_user_before(groups, k):
            if groups is prologue:
                return k - 2
            users = [n - BODY for n in range(BODY) if not loop_body[n].refilled]
            users += [n for n in range(k) if not groups[n].refilled]
            return users[-2]

        HIGH_PRO, HIGH_BODY = (sum(g.how != NATIVE for g in x) for x in (prologue, loop_body))

        def high_count(i, groups, k):
            start = 0 if groups is prologue else HIGH_PRO + HIGH_BODY * i
            return start + sum(g.how != NATIVE for g in groups[:k + 1])

        def low_count(i, groups, k):
            how = groups[k].how
            start = 0 if groups is prologue else \
                count_before(prologue, PRO, how) + count_before(loop_body, BODY, how) * i
            return start + count_before(groups, k + 1, how)

        def group_count(i, groups, k):
            return k if groups is prologue else PRO + BODY * i + k

        def ring_of(groups, k):
            return (k if groups is prologue else PRO + k) % RING

        def low_ring_of(groups, k):
            return (k if groups is prologue else PRO + k) % RING_LOW

        def rows_of(g):
            return P if g.layer == 1 else K0_LAST if g.last else K0

        def weight_tile(g, t):
            return t if g.layer == 0 else T0 + t

        def e_move(i, n):
            to, size, start = (e_stack, GCOLS, (i % 2) * GCOLS) if n < 2 else (e_copies, COLS, half_of(i, n - 2))
            dst = to[:, start:start + size] if isinstance(start, int) else to[:, bass.ds(start, size)]
            if n < 2:
                return (dst.rearrange("p (q d b) -> p d q b", q=QB, d=D)[:, 8 * n:8 * n + 8],
                        e_bank(i, n).bitcast(BF16).rearrange("p (d q b) -> p d q b", d=8, q=QB))
            return dst[0:K0], e_bank(i, n)[0:K0]

        def half_of(i, block):
            return ((i + block // QB) % 2) * GCOLS + (block % QB) * COLS

        def part_of(n):
            return e_parts[:, :, 0:PARTS * F].rearrange("p d (f n) -> p d f n", n=PARTS)[:, :, :, n]

        ids_v = ids.rearrange("(g p) f -> g p f", p=P)
        block = ctx.enter_context(nc.Block())

        @block.sync
        def _(sp):
            sp.dma_start(idx[:], ids_v[0]).then_inc(s_idx, 16)
            w0_v = W0.rearrange("o (h m) -> o h m", h=F)
            sp.dma_start(w0_in[0:H], w0_v[H:L]).then_inc(s_w0, 16)
            sp.dma_start(w0_in[H:L], w0_v[0:H]).then_inc(s_w0, 16)
            sp.dma_start(w1_in, W1.rearrange("o (h m) -> o h m", h=H)).then_inc(s_w1, 16)
            b0_v = b0.rearrange("(p a) -> p a", a=1)
            sp.dma_start(bias0[0:H], b0_v[H:L]).then_inc(s_small, 16)
            sp.dma_start(bias0[H:L], b0_v[0:H]).then_inc(s_small, 16)
            sp.dma_start(bias1[:], b1.rearrange("(p a) -> p a", a=1)).then_inc(s_small, 16)
            sp.wait_ge(s_zeroed, 2)
            sp.dma_start(dense[:, :, H:H + C], dense_ctx.rearrange("(g p) c -> p g c", p=P)).then_inc(s_top, 16)
            sp.dma_start(wt3[:], W_top3.rearrange("(p t) n -> p (t n)", p=P)).then_inc(s_top, 16)
            sp.dma_start(bias_t1[:], b_top1.rearrange("(p t) -> p t", p=P)).then_inc(s_top, 16)
            sp.dma_start(bias_t2[:], b_top2.rearrange("(p t) -> p t", p=P)).then_inc(s_top, 16)

            def next_ids(i):
                sp.wait_ge(s_gather, (i + 1) * (16 * F))
                nxt = (i + 1) % GROUPS
                row = ids_v[nxt] if isinstance(i, int) else ids_v[bass.ds(nxt, 1)].rearrange("g p f -> p (g f)")
                sp.dma_start(idx[:], row).then_inc(s_idx, 16)

            def shift_e(i, g, block):
                start = half_of(i, block)
                size = 2 * COLS if g.layer == 0 else COLS
                for t, j, rows in shifts_of(g):
                    first = (3 if g.layer == 0 else 2) * t + j
                    src = e_copies[first:first + rows, start:start + size] if isinstance(start, int) else \
                        e_copies[first:first + rows, bass.ds(start, size)]
                    to = e_shifted[j * F:(j + 1) * F, t] if g.layer == 0 else \
                        e1_shifted[j * H:(j + 1) * H, g.buffer, t - g.tiles[0]]
                    sp.dma_start(to, src).then_inc(shift_sem(g), 16)

            def refill(i, groups, k):
                g = groups[k]
                block = g.block + 1
                e_there = E_BANKS * (i + (block + 1) // QB) + 3 + (block + 1) % QB
                sp.wait_ge(s_z, group_count(i, groups, k) + 1)
                if g.layer == 0 and g.first:
                    sp.sem_inc(s_refill_go, 1)
                    sp.wait_ge(s_eout, e_there)
                shift_e(i, g, block)

            next_ids(0)
            for g in loop_body[0:PAIRS1 + PAIRS0]:
                if g.refilled:
                    sp.wait_ge(s_eout, E_BANKS if g.layer == 0 else 3)
                    shift_e(0, g, g.block)

            def body(i, groups):
                for k, g in enumerate(groups):
                    if g.refilled and not (groups is last_body and g.block == QB - 1) \
                            and (g.layer == 1 or g.block % 2):
                        refill(i, groups, k)
                    if groups is loop_body and k == IDS_STEP:
                        next_ids(i + 1)

            with sp.Fori(0, GROUPS - 1) as i:
                body(i, loop_body)
            body(GROUPS - 1, last_body)
            last0 = max(k for k, g in enumerate(last_body) if g.layer == 0)
            sp.wait_ge(s_z, group_count(GROUPS - 1, last_body, last0) + 1)
            sp.dma_start(wt1_a[0:H], W_top1[0:H]).then_inc(s_wtop, 16)
            sp.dma_start(wt1_a[H:H + C], W_top1[H + L:H + L + C]).then_inc(s_wtop, 16)
            sp.dma_start(wt1_b, W_top1[H:H + L]).then_inc(s_wtop, 16)
            sp.dma_start(wt2, W_top2.rearrange("(p t) n -> p t n", p=P)).then_inc(s_wtop, 16)
            sp.wait_ge(s_idx, 16 * (GROUPS + 1))
            sp.wait_ge(s_gather, 16 * (F * GROUPS + EARLY))
            sp.wait_ge(s_mlp_act, 14)
            sp.dma_start(out.rearrange("b a -> a b"), y_row[:]).then_inc(s_out, 16)
            sp.wait_ge(s_out, 16)

        @block.gpsimd
        def _(pool):
            for tile in (ident, ident_bf, pick):
                pool.memset(tile[:], 0.0).then_inc(s_const, 1)
            pool.wait_ge(s_const, 3)
            for tile in (ident, ident_bf):
                pool.affine_select(out=tile[:], in_=tile[:], compare_op=ALU.not_equal, fill=1.0, base=0,
                                   pattern=[[-1, P]], channel_multiplier=1).then_inc(s_const, 1)
            for part in range(PARTS):
                pool.wait_ge(s_const, 5 + part)
                pool.affine_select(out=pick[:], in_=pick[:], compare_op=ALU.not_equal,
                                   fill=1.0, base=-part, pattern=[[-PARTS, F]],
                                   channel_multiplier=1).then_inc(s_const, 1)

            def gather(f):
                pool.indirect_dma_start(gathered[:, f, :], None, tables[f],
                                        bass.IndirectOffsetOnAxis(idx[:, f:f + 1].bitcast(U32), 0)
                                        ).then_inc(s_gather, 16)

            def low_part(i, groups, k):
                g = groups[k]
                r, n, rows = ring_of(groups, k), len(g.tiles), rows_of(g)
                if not (groups is prologue and k < RING_LOW):
                    pool.wait_ge(s_main, group_count(i, groups, k) - RING_LOW + 1)
                pool.wait_ge(s_high, high_count(i, groups, k))
                pool.tensor_tensor(z_low[0:rows, low_ring_of(groups, k), 0:n], z[0:rows, r, 0:n],
                                   z_high[0:rows, r, 0:n].bitcast(F32), ALU.subtract).then_inc(s_low_pool, 1)

            pool.wait_ge(s_idx, 16)
            for f in range(F):
                gather(f)

            def start_gathers(i):
                pool.wait_ge(s_idx, 16 * (i + 1))
                pool.wait_ge(s_eprep_dve, 2 * i)
                pool.sem_inc(s_gather_go, 1)

            start_gathers(1)
            for f in range(EARLY):
                gather(f)

            def body(i, groups):
                for k, g in enumerate(groups):
                    if g.how == BY_POOL:
                        low_part(i, groups, k)
                    if groups is loop_body:
                        if k == E_STEP + 1:
                            start_gathers(i + 2)
                        for f in GATHERS.get(k, ()):
                            gather(f)

            with pool.Fori(0, GROUPS - 1) as i:
                body(i, loop_body)
            body(GROUPS - 1, last_body)
            pool.wait_ge(s_wt2_high, 1)
            pool.tensor_tensor(wt2_part(True), wt2, wt2_part(False).bitcast(F32), ALU.subtract).then_inc(s_wt2_low, 1)
            for hf in range(2):
                for t in range(0, M1 // P, 2):
                    n = hf * (M1 // P) + t
                    pool.wait_ge(s_h1_high, n + 1)
                    pool.tensor_tensor(mlp_h1_part(hf, t, True), mlp_h1(hf, t),
                                       mlp_h1_part(hf, t, False).bitcast(F32), ALU.subtract).then_inc(s_h1_low_pool, 1)

        @block.scalar
        def _(act):
            def e_split(i, step):
                if step == 0:
                    act.wait_ge(s_gather, (16 * F) * (i + 1))
                    act.activation(part_of(0), gathered[:].rearrange("p f d -> p d f"), ACT.Copy).then_inc(s_eprep_act, 1)
                else:
                    act.wait_ge(s_eprep_dve, 2 * i + 1)
                    act.activation(part_of(1), gathered[:].rearrange("p f d -> p d f"), ACT.Copy).then_inc(s_eprep_act, 1)

            def e_out(i, n):
                act.wait_ge(s_etr, E_BANKS * i + n + 1)
                dst, src = e_move(i, n)
                act.activation(dst, src, ACT.Copy).then_inc(s_eout, 1)

            def high_part(i, groups, k):
                g = groups[k]
                if g.how == NATIVE:
                    return
                r, n, rows = ring_of(groups, k), len(g.tiles), rows_of(g)
                act.wait_ge(s_z, group_count(i, groups, k) + 1)
                act.activation(z_high[0:rows, r, 0:n], z[0:rows, r, 0:n], ACT.Copy).then_inc(s_high, 1)

            def read_sums0(c_even, done):
                b = c_even
                act.wait_ge(s_main, done)
                act.activation(hidden[H:L, b], acc[0][H:L], ACT.Relu, bias=bias0[H:L]).then_inc(s_read0, 1)
                act.activation(relu0[:], acc[0][0:H], ACT.Relu, bias=bias0[0:H]).then_inc(s_read0, 1)

            def copy_hidden(b, done):
                act.wait_ge(s_read0, done)
                act.activation(hidden[0:H, b], hidden[H:L, b], ACT.Copy).then_inc(s_hid, 1)

            def read_sums1(done):
                act.wait_ge(s_main, done)
                act.activation(relu1[:], acc[1], ACT.Relu, bias=bias1[:]).then_inc(s_read1, 1)

            act.wait_ge(s_w1, 16)
            for h0, h1, wide in w1_wide:
                to = wide.rearrange("p (h m) -> p h m", m=WIDE1)
                act.activation(to[:, :, 0:F], w1_in[:, h0:h1], ACT.Copy)
                act.activation(to[:, :, F:WIDE1], w1_in[:, h0:h1, 0:WIDE1 - F], ACT.Copy).then_inc(s_w1_rows, 1)
            for n, (h0, h1, wide) in enumerate(w1_wide):
                act.wait_ge(s_w1_rows, n + 1)
                windows = bass.AP(wide.tensor, wide.offset, [wide.ap[0], [1, F], [WIDE1 + 1, h1 - h0]])
                act.activation(w1_rows.rearrange("p (s h) -> p s h", h=H)[:, :, h0:h1], windows,
                               ACT.Copy).then_inc(s_w1_rows, 1)
            act.wait_ge(s_zeroed, 6)
            for n, (w, cnt, rows) in enumerate(WBANKS):
                act.wait_ge(s_wt, n + 1)
                for rr, c0, cc in rows:
                    ins = act.activation(w_high[0:rr, w + c0:w + c0 + cc], wbank(n)[0:rr, c0:c0 + cc], ACT.Copy)
                ins.then_inc(s_wt_high, 1)
            act.wait_ge(s_small, 48)
            act.nop().then_inc(s_read1, 1)
            act.wait_ge(s_dense_t, 1)
            dv = top_a[H:H + C].rearrange("c (x b) -> c x b", x=2)
            act.activation(dv[:, 0], misc[0][H:H + C], ACT.Copy).then_inc(s_dense, 1)
            act.activation(dv[:, 1], misc[1][H:H + C], ACT.Copy).then_inc(s_dense, 1)
            e_split(0, 0)
            e_split(0, 1)
            for n in (0, 2, 3):
                e_out(0, n)

            after = ACT_AFTER
            for k, g in enumerate(prologue):
                high_part(0, prologue, k)
                if k == 2:
                    for n in range(4, E_BANKS):
                        e_out(0, n)
                if k - after >= 0 and prologue[k - after].last:
                    read_sums0(0, k - after + 1)
                    copy_hidden(0, 1)

            def body(i, groups):
                for k, g in enumerate(groups):
                    high_part(i, groups, k)
                    if k == after - 1:
                        act.wait_ge(s_sum0, i * QB + 1)
                        read_sums0(1, group_count(i, groups, 0))
                        copy_hidden(1, 2 * (i * QB + 2) - 1)
                    j = k - after
                    if j >= 0 and groups[j].last:
                        done = group_count(i, groups, j) + 1
                        if groups[j].layer == 1:
                            read_sums1(done)
                        else:
                            c = groups[j].block
                            read_sums0(c % 2, done)
                            copy_hidden(c % 2, 2 * (i * QB + c + 1) - 1)
                    if groups is loop_body:
                        if k == E_STEP:
                            e_split(i + 1, 0)
                        if k == E_STEP + E_REST:
                            e_split(i + 1, 1)
                        if k in E_OUT:
                            for n in E_OUT[k]:
                                e_out(i + 1, n)

            with act.Fori(0, GROUPS - 1) as i:
                body(i, loop_body)
            body(GROUPS - 1, last_body)
            read_sums1(group_count(GROUPS - 1, last_body, len(last_body)))
            act.wait_ge(s_wtop, 64)
            act.activation(wt2_part(False), wt2, ACT.Copy).then_inc(s_wt2_high, 1)

            for n in range(M1 // P * 2):
                hf, t = divmod(n, M1 // P)
                act.wait_ge(s_mlp, n + 1)
                act.activation(mlp_h1(hf, t), mlp_bank(n), ACT.Relu, bias=bias_t1[:, t:t + 1]).then_inc(s_mlp_act, 1)
            for n in range(M2 // P * 2):
                hf, t = divmod(n, M2 // P)
                act.wait_ge(s_mlp, 8 + n + 1)
                act.activation(mlp_h2(hf, t), mlp_bank(n), ACT.Relu, bias=bias_t2[:, t:t + 1]).then_inc(s_mlp_act, 1)
            for hf in range(2):
                act.wait_ge(s_mlp, 12 + hf + 1)
                act.activation(y_row[0:1, hf * 512:(hf + 1) * 512], mlp_bank(4 + hf)[0:1], ACT.Copy).then_inc(s_mlp_act, 1)

        @block.vector
        def _(dve):
            dve.memset(e_parts[:], 0.0).then_inc(s_zeroed, 1)
            dve.memset(dense, 0.0).then_inc(s_zeroed, 1)
            dve.memset(ones[:], 1.0).then_inc(s_zeroed, 1)
            for w in (w_full, w_high, w_low):
                dve.memset(w[:, T0 + T1 - 1].bitcast(F32), 0.0).then_inc(s_zeroed, 1)
            dve.wait_ge(s_w0, 32)
            sym = w0_sym.rearrange("p (h m) -> p h m", m=WIDE)
            dve.tensor_tensor(sym[:, :, 0:F], w0_in, w0_in.rearrange("p h m -> p m h"), ALU.add).then_inc(s_sym, 1)
            diagonal = w0_sym[:, 0:(WIDE + 1) * (F - 1) + 1:WIDE + 1]
            dve.wait_ge(s_sym, 1)
            dve.tensor_scalar(diagonal, diagonal, 0.5, None, ALU.mult).then_inc(s_sym, 1)
            dve.wait_ge(s_sym, 2)
            dve.tensor_copy(sym[:, :, F:WIDE], sym[:, :, 0:WIDE - F]).then_inc(s_sym, 1)
            dve.wait_ge(s_sym, 3)
            windows = bass.AP(w0_sym.tensor, w0_sym.offset, [w0_sym.ap[0], [1, SHIFTS], [WIDE + 1, F]])
            dve.tensor_copy(w0_rows.rearrange("p (s h) -> p s h", h=F), windows).then_inc(s_sym, 1)
            dve.wait_ge(s_const, 5 + PARTS)
            dve.tensor_copy(pick_wide[:], pick[:].rearrange("p (o f) -> p o f", o=1)
                            .broadcast_to([P, 3, F])).then_inc(s_pick, 1)
            dve.wait_ge(s_pick, 1)
            for run in runs1:
                n, at1 = len(run), picked1.index(run[0])
                shifted_columns = bass.AP(pick_wide, 2 * run[0], [[3 * F, P], [1, 2 * n], [1, H]])
                dve.tensor_copy(pick1[:, at1:at1 + n].rearrange("p t j h -> p (t j) h"), shifted_columns) \
                   .then_inc(s_pick, 1)
            shifted_columns = bass.AP(pick_wide, 0, [[3 * F, P], [1, 3 * T0], [1, F]])
            dve.tensor_copy(pick0, shifted_columns).then_inc(s_pick, 1)
            dve.wait_ge(s_zeroed, 6)
            for n, (w, cnt, rows) in enumerate(WBANKS):
                dve.wait_ge(s_wt_high, n + 1)
                for rr, c0, cc in rows:
                    dve.tensor_copy(w_full[0:rr, w + c0:w + c0 + cc], wbank(n)[0:rr, c0:c0 + cc])
                    ins = dve.tensor_tensor(w_low[0:rr, w + c0:w + c0 + cc], wbank(n)[0:rr, c0:c0 + cc],
                                            w_high[0:rr, w + c0:w + c0 + cc].bitcast(F32), ALU.subtract)
                ins.then_inc(s_wt_low, 1)

            def e_rest_of(i, step):
                if step == 0:
                    dve.wait_ge(s_eprep_act, 2 * i + 1)
                    rest = gathered[:].rearrange("p f d -> p d f")
                    dve.tensor_tensor(rest, rest, part_of(0), ALU.subtract).then_inc(s_eprep_dve, 1)
                else:
                    dve.wait_ge(s_eprep_act, 2 * i + 2)
                    dve.tensor_tensor(part_of(2), gathered[:].rearrange("p f d -> p d f"), part_of(1),
                                      ALU.subtract).then_inc(s_eprep_dve, 1)

            def form_z(i, groups, k):
                g = groups[k]
                r, n, rows = ring_of(groups, k), len(g.tiles), rows_of(g)
                if not (groups is prologue and k < RING):
                    dve.wait_ge(s_main, group_count(i, groups, k) - RING + 1)
                if g.layer == 1 and g.first:
                    dve.wait_ge(s_hid, i * QB + g.block + 1)
                if g.layer == 1:
                    kept = hidden[:, g.block % 2]
                if g.refilled:
                    fills = i * QB + g.block + 1 if g.layer else i * (QB // 2) + g.block // 2
                    dve.wait_ge(shift_sem(g), 16 * len(shifts_of(g)) * fills)
                    other = e1_shifted[:, g.buffer, 0:n] if g.layer else \
                        e_shifted[0:rows, g.tiles[0]:g.tiles[-1] + 1, g.block % 2 * COLS:(g.block % 2 + 1) * COLS]
                else:
                    slot = spread_before(groups, k) % 2
                    dve.wait_ge(s_spread, spread_count(i, groups, k) + 1)
                    other = spread[slot][0:rows, 0:n * COLS].rearrange("p (t c) -> p t c", t=n)
                if g.layer == 0:
                    if groups is prologue and g.first:
                        dve.wait_ge(s_eout, 3 + g.block)
                    start = half_of(i, g.block)
                    kept = e_copies[0:rows, start:start + COLS] if isinstance(start, int) else \
                        e_copies[0:rows, bass.ds(start, COLS)]
                kept = kept.rearrange("p (o c) -> p o c", o=1).broadcast_to([rows, n, COLS])
                dve.tensor_tensor(z[0:rows, r, 0:n], other, kept, ALU.mult).then_inc(s_z, 1)

            def low_part(i, groups, k):
                g = groups[k]
                if g.how != BY_DVE:
                    return
                r, n, rows = ring_of(groups, k), len(g.tiles), rows_of(g)
                if not (groups is prologue and k < RING_LOW):
                    dve.wait_ge(s_main, group_count(i, groups, k) - RING_LOW + 1)
                dve.wait_ge(s_high, high_count(i, groups, k))
                dve.tensor_tensor(z_low[0:rows, low_ring_of(groups, k), 0:n], z[0:rows, r, 0:n],
                                  z_high[0:rows, r, 0:n].bitcast(F32), ALU.subtract).then_inc(s_low_dve, 1)

            def sum_dims(layer, done, column):
                src, rows, to = (relu0, H, top_a) if layer == 0 else (relu1, P, top_b)
                dve.wait_ge(s_read0 if layer == 0 else s_read1, done)
                dst = to[0:rows, column:column + RB] if isinstance(column, int) else to[0:rows, bass.ds(column, RB)]
                dve.tensor_reduce(dst, src[:].rearrange("p (d b) -> p b d", d=D), AX_X, ALU.add) \
                   .then_inc(s_sum0 if layer == 0 else s_sum1, 1)

            e_rest_of(0, 0)
            e_rest_of(0, 1)
            dve.wait_ge(s_etr, 2)
            dst, src = e_move(0, 1)
            dve.tensor_copy(dst, src).then_inc(s_eout, 1)
            for k in range(PRO):
                form_z(0, prologue, k)
                if k:
                    low_part(0, prologue, k - 1)
                if k == PRO - 1:
                    sum_dims(0, 2, 0)
            after = DVE_AFTER

            def body(i, groups):
                for k, g in enumerate(groups):
                    form_z(i, groups, k)
                    if k:
                        low_part(i, groups, k - 1)
                    if k == after:
                        sum_dims(0, 2 * (i * QB + 2), i * P + RB)
                    j = k - after
                    if j >= 0 and groups[j].last:
                        c = groups[j].block
                        if groups[j].layer == 1:
                            sum_dims(1, i * QB + c + 2, i * P + c * RB)
                        elif c <= QB:
                            sum_dims(0, 2 * (i * QB + c + 1), i * P + c * RB)
                    if groups is loop_body:
                        if k == E_STEP + 1:
                            e_rest_of(i + 1, 0)
                        if k == E_STEP + E_REST + 1:
                            e_rest_of(i + 1, 1)
                low_part(i, groups, len(groups) - 1)

            with dve.Fori(0, GROUPS - 1) as i:
                body(i, loop_body)
            body(GROUPS - 1, last_body)
            c = GROUPS * QB - 1
            sum_dims(1, c + 2, c * RB)
            for hf in range(2):
                for t in range(M1 // P):
                    n = hf * (M1 // P) + t
                    dve.wait_ge(s_mlp_act, n + 1)
                    dve.tensor_copy(mlp_h1_part(hf, t, False), mlp_h1(hf, t)).then_inc(s_h1_high, 1)
                    if t % 2:
                        dve.wait_ge(s_h1_high, n + 1)
                        dve.tensor_tensor(mlp_h1_part(hf, t, True), mlp_h1(hf, t),
                                          mlp_h1_part(hf, t, False).bitcast(F32), ALU.subtract).then_inc(s_h1_low, 1)
            for hf in range(2):
                for t in range(M2 // P):
                    dve.wait_ge(s_mlp_act, 8 + hf * (M2 // P) + t + 1)
                    if t == 0:
                        dve.tensor_scalar(mlp_weighted(hf, 0), mlp_h2(hf, 0), wt3[:, 0:1], None,
                                          ALU.mult).then_inc(s_weighted, 1)
                    else:
                        dve.wait_ge(s_weighted, hf * (M2 // P) + t)
                        dve.scalar_tensor_tensor(mlp_weighted(hf, t), mlp_h2(hf, t), wt3[:, t:t + 1],
                                                 mlp_weighted(hf, t - 1), ALU.mult, ALU.add).then_inc(s_weighted, 1)

        @block.tensor
        def _(pe):
            pe.wait_ge(s_const, 5)
            pe.wait_ge(s_sym, 4)
            for n, (w, cnt, rows) in enumerate(WBANKS):
                if n == 2:
                    pe.wait_ge(s_w1_rows, 4)
                if n >= 4:
                    pe.wait_ge(s_wt_low, n - 3)
                for t in range(cnt):
                    if w < T0:
                        c, size = (w + t) * K0, K0 if w + t < T0 - 1 else K0_LAST
                        src = w0_rows[:, c:c + size]
                    else:
                        c = (w - T0 + t) * P
                        size = min(P, H * F - c)
                        src = w1_rows[:, c:c + size]
                    ins = pe.transpose(wbank(n)[0:size, t], src, ident[:])
                ins.then_inc(s_wt, 1)

            pe.wait_ge(s_top, 64)
            for gi in range(GROUPS):
                ins = pe.transpose(misc[gi // 4][0:H + C, (gi % 4) * P:(gi % 4 + 1) * P], dense[:, gi], ident[:])
            ins.then_inc(s_dense_t, 1)

            def e_fill(i, n):
                out = e_bank(i, n)
                if isinstance(i, int) and n == 0:
                    pe.wait_ge(s_wt_low, len(WBANKS))
                if isinstance(i, int) and n == 2:
                    pe.wait_ge(s_dense, 2)
                if n >= 2:
                    pe.wait_ge(s_eout, E_BANKS * i + max(n - 1, 2))
                elif not isinstance(i, int):
                    pe.wait_ge(s_eout, E_BANKS * i + n - 1)
                if n < 2:
                    pe.wait_ge(s_eprep_dve, 2 * i + 2)
                    for d in range(8):
                        ins = pe.transpose(out.bitcast(BF16)[:, d * P:(d + 1) * P], e_parts[:, 8 * n + d], ident_bf[:])
                else:
                    start = half_of(i, n - 2)
                    moving = e_stack[:, start:start + COLS] if isinstance(start, int) else e_stack[:, bass.ds(start, COLS)]
                    ins = pe.matmul(out[0:K0], pick_wide[:].rearrange("p j f -> p (j f)"), moving, start=True, stop=True)
                ins.then_inc(s_etr, 1)

            def spread_group(i, groups, k):
                g = groups[k]
                if g.refilled:
                    return
                slot = spread_before(groups, k) % 2
                if groups is loop_body and isinstance(i, int) and i == 0 and spread_before(groups, k) < 2:
                    pe.wait_ge(s_z, PRO - 1 + spread_before(groups, k))
                elif groups is not prologue or k >= 2:
                    before = slot_user_before(groups, k)
                    pe.wait_ge(s_z, group_count(i, groups, before) + 1)
                if g.first and g.block == 0:
                    pe.wait_ge(s_eout, E_BANKS * i + 2)
                start = half_of(i, g.block)
                moving = e_stack[:, start:start + COLS] if isinstance(start, int) else e_stack[:, bass.ds(start, COLS)]
                for x, t in enumerate(g.tiles):
                    rows = K0 if g.layer == 0 else P
                    chosen = pick0[:, 3 * t:3 * t + 3] if g.layer == 0 else pick1[:, picked1.index(t)]
                    ins = pe.matmul(spread[slot][0:rows, x * COLS:(x + 1) * COLS],
                                    chosen.rearrange("p j h -> p (j h)"), moving, start=True, stop=True)
                ins.then_inc(s_spread, 1)

            def multiply(i, groups, k):
                g = groups[k]
                r = ring_of(groups, k)
                if g.first and not (groups is prologue and k == 0):
                    c = i * QB + g.block
                    if g.layer == 0:
                        pe.wait_ge(s_read0, 2 * c)
                    else:
                        pe.wait_ge(s_read1, c + 1)
                r_low = low_ring_of(groups, k)
                passes = [(w_full, z, r, s_z, group_count(i, groups, k) + 1)]
                if g.how != NATIVE:
                    low = s_low_dve if g.how == BY_DVE else s_low_pool
                    passes = [(w_high, z_high, r, s_high, high_count(i, groups, k)),
                              (w_low, z_high, r, None, None),
                              (w_high, z_low, r_low, low, low_count(i, groups, k))]
                for n, (w, moving, slot, ready, value) in enumerate(passes):
                    if ready is not None:
                        pe.wait_ge(ready, value)
                    for x, t in enumerate(g.tiles):
                        kk = rows_of(g)
                        ins = pe.matmul(acc[g.layer], w[0:kk, weight_tile(g, t)], moving[0:kk, slot, x],
                                        start=g.first and n == 0 and x == 0,
                                        stop=g.last and n == len(passes) - 1 and x == len(g.tiles) - 1)
                ins.then_inc(s_main, 1)

            for n in range(4):
                e_fill(0, n)
            pe.wait_ge(s_pick, 2 + len(runs1))

            for k in range(LEAD):
                spread_group(0, prologue, k)
            for k in range(PRO):
                if k + LEAD < PRO:
                    spread_group(0, prologue, k + LEAD)
                else:
                    spread_group(0, loop_body, k + LEAD - PRO)
                multiply(0, prologue, k)
                if k == 0:
                    for n in range(4, E_BANKS):
                        e_fill(0, n)

            def body(i, groups):
                for k in range(len(groups)):
                    if k + LEAD < len(groups):
                        spread_group(i, groups, k + LEAD)
                    elif groups is loop_body:
                        spread_group(i + 1, loop_body, k + LEAD - BODY)
                    multiply(i, groups, k)
                    if groups is loop_body and k in E_FILL:
                        for n in E_FILL[k]:
                            e_fill(i + 1, n)

            with pe.Fori(0, GROUPS - 1) as i:
                body(i, loop_body)
            body(GROUPS - 1, last_body)

            for hf in range(2):
                if hf == 0:
                    pe.wait_ge(s_dense, 2)
                    pe.wait_ge(s_wtop, 64)
                pe.wait_ge(s_sum1, (hf + 1) * GROUPS * QB // 2)
                pe.wait_ge(s_sum0, (hf + 1) * GROUPS * QB // 2)
                for t in range(M1 // P):
                    o = mlp_bank(hf * (M1 // P) + t)
                    pe.matmul(o, wt1_a[:, t::M1 // P], top_a[:, hf * N:(hf + 1) * N], start=True, stop=False)
                    pe.matmul(o, wt1_b[:, t::M1 // P], top_b[:, hf * N:(hf + 1) * N],
                              start=False, stop=True).then_inc(s_mlp, 1)
            pe.wait_ge(s_wt2_low, 1)
            for hf in range(2):
                pe.wait_ge(s_mlp_act, (hf + 1) * (M2 // P))
                for kt in range(M1 // P):
                    n = hf * (M1 // P) + kt + 1
                    pe.wait_ge(s_h1_high, n)
                    for t in range(M2 // P):
                        for low in (False, True):
                            pe.matmul(mlp_bank(hf * (M2 // P) + t), wt2_part(low)[:, kt, t::M2 // P],
                                      mlp_h1_part(hf, kt, False),
                                      start=kt == 0 and not low, stop=False)
                for t in range(M2 // P):
                    for kt in range(M1 // P):
                        if t == 0:
                            n = (hf * (M1 // P) + kt) // 2 + 1
                            pe.wait_ge(s_h1_low if kt % 2 else s_h1_low_pool, n)
                        ins = pe.matmul(mlp_bank(hf * (M2 // P) + t), wt2_part(False)[:, kt, t::M2 // P],
                                        mlp_h1_part(hf, kt, True), start=False, stop=kt == M1 // P - 1)
                    ins.then_inc(s_mlp, 1)
            for hf in range(2):
                pe.wait_ge(s_weighted, (M2 // P) * (hf + 1))
                pe.matmul(mlp_bank(4 + hf)[0:1], ones[:], mlp_weighted(hf, M2 // P - 1),
                          start=True, stop=True).then_inc(s_mlp, 1)


def kernel(**inputs):
    import numpy as np
    import concourse.bacc as bacc
    from concourse.bass_utils import run_bass_kernel_spmd

    nc = bacc.Bacc("TRN2", target_bir_lowering=False, num_devices=1)
    arrays, aps = {}, {}
    for name, value in inputs.items():
        a = np.ascontiguousarray(value)
        arrays[f"in_{name}"] = a
        aps[name] = nc.dram_tensor(f"in_{name}", a.shape, mybir.dt.from_np(a.dtype), kind="ExternalInput").ap()
    rows, fields = inputs["ids"].shape
    out = nc.dram_tensor("out_y", (rows, 1), F32, kind="ExternalOutput").ap()
    dlrm_kernel(nc, aps["dense_ctx"], aps["ids"], [aps[f"tbl_{f}"] for f in range(fields)],
                aps["W_top1"], aps["b_top1"], aps["W_top2"], aps["b_top2"], aps["W_top3"],
                aps["L0_rec_W0"], aps["L0_rec_b0"], aps["L0_rec_W1"], aps["L0_rec_b1"], out)
    r = run_bass_kernel_spmd(nc, [arrays], core_ids=[0])
    return r.results[0]["out_y"]
```
